# Optimizing a Trainium2 kernel written in Bass

```python
import numpy as np
import jax
import jax.numpy as jnp

def _softmax(x, axis=-1):
    return jax.nn.softmax(x, axis=axis)

def _gelu(x):
    return jax.nn.gelu(x, approximate=True)

def _silu(x):
    return jax.nn.silu(x)

def _sigmoid(x):
    return jax.nn.sigmoid(x)

def _layernorm(x, axis=-1, eps=1e-05):
    m = jnp.mean(x, axis=axis, keepdims=True)
    v = jnp.var(x, axis=axis, keepdims=True)
    return (x - m) / jnp.sqrt(v + eps)

def _scatter_add(tgt, idx, src, axis=0):
    return tgt.at[idx].add(src)

def _segment_sum(src, seg, n):
    return jax.ops.segment_sum(src, seg, n)
kernel_name = 'mk_dlrm_tower_d1_rec_r8_ae8b43'

def setup_inputs(seed: int=0):
    np.random.seed(seed)
    _w = jnp.asarray

    def _rec_inputs():
        import jax
        import jax.numpy as jnp
        _tk = jax.random.key(seed)
        dense_ctx = jax.random.normal(jax.random.fold_in(_tk, 190), (512, 16), jnp.float32)
        ids = jnp.stack([jax.random.randint(jax.random.fold_in(_tk, 200 + f), (512,), 0, v, jnp.int32) for f, v in enumerate([12500, 12500, 1000, 1250, 1250, 1000, 1250, 125000, 125000, 1000, 125000, 125000, 1250, 125000, 1250, 1000, 1250, 12500, 1000, 12500, 125000, 1250, 1250, 12500, 1000, 1000, 12500, 1250, 12500, 125000, 125000, 12500, 125000, 125000, 1250, 12500, 12500, 1250, 1000])], axis=1)
        tbl_0 = 0.05 * jax.random.normal(jax.random.fold_in(_tk, 500 + 0), (12500, 16), jnp.float32)
        tbl_1 = 0.05 * jax.random.normal(jax.random.fold_in(_tk, 500 + 1), (12500, 16), jnp.float32)
        tbl_2 = 0.05 * jax.random.normal(jax.random.fold_in(_tk, 500 + 2), (1000, 16), jnp.float32)
        tbl_3 = 0.05 * jax.random.normal(jax.random.fold_in(_tk, 500 + 3), (1250, 16), jnp.float32)
        tbl_4 = 0.05 * jax.random.normal(jax.random.fold_in(_tk, 500 + 4), (1250, 16), jnp.float32)
        tbl_5 = 0.05 * jax.random.normal(jax.random.fold_in(_tk, 500 + 5), (1000, 16), jnp.float32)
        tbl_6 = 0.05 * jax.random.normal(jax.random.fold_in(_tk, 500 + 6), (1250, 16), jnp.float32)
        tbl_7 = 0.05 * jax.random.normal(jax.random.fold_in(_tk, 500 + 7), (125000, 16), jnp.float32)
        tbl_8 = 0.05 * jax.random.normal(jax.random.fold_in(_tk, 500 + 8), (125000, 16), jnp.float32)
        tbl_9 = 0.05 * jax.random.normal(jax.random.fold_in(_tk, 500 + 9), (1000, 16), jnp.float32)
        tbl_10 = 0.05 * jax.random.normal(jax.random.fold_in(_tk, 500 + 10), (125000, 16), jnp.float32)
        tbl_11 = 0.05 * jax.random.normal(jax.random.fold_in(_tk, 500 + 11), (125000, 16), jnp.float32)
        tbl_12 = 0.05 * jax.random.normal(jax.random.fold_in(_tk, 500 + 12), (1250, 16), jnp.float32)
        tbl_13 = 0.05 * jax.random.normal(jax.random.fold_in(_tk, 500 + 13), (125000, 16), jnp.float32)
        tbl_14 = 0.05 * jax.random.normal(jax.random.fold_in(_tk, 500 + 14), (1250, 16), jnp.float32)
        tbl_15 = 0.05 * jax.random.normal(jax.random.fold_in(_tk, 500 + 15), (1000, 16), jnp.float32)
        tbl_16 = 0.05 * jax.random.normal(jax.random.fold_in(_tk, 500 + 16), (1250, 16), jnp.float32)
        tbl_17 = 0.05 * jax.random.normal(jax.random.fold_in(_tk, 500 + 17), (12500, 16), jnp.float32)
        tbl_18 = 0.05 * jax.random.normal(jax.random.fold_in(_tk, 500 + 18), (1000, 16), jnp.float32)
        tbl_19 = 0.05 * jax.random.normal(jax.random.fold_in(_tk, 500 + 19), (12500, 16), jnp.float32)
        tbl_20 = 0.05 * jax.random.normal(jax.random.fold_in(_tk, 500 + 20), (125000, 16), jnp.float32)
        tbl_21 = 0.05 * jax.random.normal(jax.random.fold_in(_tk, 500 + 21), (1250, 16), jnp.float32)
        tbl_22 = 0.05 * jax.random.normal(jax.random.fold_in(_tk, 500 + 22), (1250, 16), jnp.float32)
        tbl_23 = 0.05 * jax.random.normal(jax.random.fold_in(_tk, 500 + 23), (12500, 16), jnp.float32)
        tbl_24 = 0.05 * jax.random.normal(jax.random.fold_in(_tk, 500 + 24), (1000, 16), jnp.float32)
        tbl_25 = 0.05 * jax.random.normal(jax.random.fold_in(_tk, 500 + 25), (1000, 16), jnp.float32)
        tbl_26 = 0.05 * jax.random.normal(jax.random.fold_in(_tk, 500 + 26), (12500, 16), jnp.float32)
        tbl_27 = 0.05 * jax.random.normal(jax.random.fold_in(_tk, 500 + 27), (1250, 16), jnp.float32)
        tbl_28 = 0.05 * jax.random.normal(jax.random.fold_in(_tk, 500 + 28), (12500, 16), jnp.float32)
        tbl_29 = 0.05 * jax.random.normal(jax.random.fold_in(_tk, 500 + 29), (125000, 16), jnp.float32)
        tbl_30 = 0.05 * jax.random.normal(jax.random.fold_in(_tk, 500 + 30), (125000, 16), jnp.float32)
        tbl_31 = 0.05 * jax.random.normal(jax.random.fold_in(_tk, 500 + 31), (12500, 16), jnp.float32)
        tbl_32 = 0.05 * jax.random.normal(jax.random.fold_in(_tk, 500 + 32), (125000, 16), jnp.float32)
        tbl_33 = 0.05 * jax.random.normal(jax.random.fold_in(_tk, 500 + 33), (125000, 16), jnp.float32)
        tbl_34 = 0.05 * jax.random.normal(jax.random.fold_in(_tk, 500 + 34), (1250, 16), jnp.float32)
        tbl_35 = 0.05 * jax.random.normal(jax.random.fold_in(_tk, 500 + 35), (12500, 16), jnp.float32)
        tbl_36 = 0.05 * jax.random.normal(jax.random.fold_in(_tk, 500 + 36), (12500, 16), jnp.float32)
        tbl_37 = 0.05 * jax.random.normal(jax.random.fold_in(_tk, 500 + 37), (1250, 16), jnp.float32)
        tbl_38 = 0.05 * jax.random.normal(jax.random.fold_in(_tk, 500 + 38), (1000, 16), jnp.float32)
        _rk = jax.random.fold_in(_tk, 7)
        W_top1 = 0.05 * jax.random.normal(jax.random.fold_in(_tk, 801), (400, 512), jnp.float32)
        W_top2 = 0.0441942 * jax.random.normal(jax.random.fold_in(_tk, 802), (512, 256), jnp.float32)
        W_top3 = 0.0625 * jax.random.normal(jax.random.fold_in(_tk, 803), (256, 1), jnp.float32)
        b_top1 = jnp.zeros((512,), jnp.float32)
        b_top2 = jnp.zeros((256,), jnp.float32)
        return (dense_ctx, ids, tbl_0, tbl_1, tbl_2, tbl_3, tbl_4, tbl_5, tbl_6, tbl_7, tbl_8, tbl_9, tbl_10, tbl_11, tbl_12, tbl_13, tbl_14, tbl_15, tbl_16, tbl_17, tbl_18, tbl_19, tbl_20, tbl_21, tbl_22, tbl_23, tbl_24, tbl_25, tbl_26, tbl_27, tbl_28, tbl_29, tbl_30, tbl_31, tbl_32, tbl_33, tbl_34, tbl_35, tbl_36, tbl_37, tbl_38, W_top1, b_top1, W_top2, b_top2, W_top3)
    dense_ctx, ids, tbl_0, tbl_1, tbl_2, tbl_3, tbl_4, tbl_5, tbl_6, tbl_7, tbl_8, tbl_9, tbl_10, tbl_11, tbl_12, tbl_13, tbl_14, tbl_15, tbl_16, tbl_17, tbl_18, tbl_19, tbl_20, tbl_21, tbl_22, tbl_23, tbl_24, tbl_25, tbl_26, tbl_27, tbl_28, tbl_29, tbl_30, tbl_31, tbl_32, tbl_33, tbl_34, tbl_35, tbl_36, tbl_37, tbl_38, W_top1, b_top1, W_top2, b_top2, W_top3 = _rec_inputs()

    def _L0_rec_setup():
        import jax, jax.numpy as jnp
        import numpy as np
        B, F0, D = (512, 39, 16)
        CIN = [128, 128, 128]

        def _cin_layer(X0, Xi, W, b):
            H = W.shape[0]
            F0_, Fi = (X0.shape[1], Xi.shape[1])
            Wr = W.reshape(H, F0_, Fi)
            return jnp.einsum('hjk,bjd,bkd->bhd', Wr, X0, Xi) + b[None, :, None]
        key = jax.random.key(seed)
        ks = jax.random.split(key, 4)
        x = jax.random.normal(ks[0], (B, F0, D), dtype=jnp.float32)
        fields = [F0] + CIN
        inp = {'embedded_features': x}
        for i in range(len(CIN)):
            cin = F0 * fields[i]
            cout = fields[i + 1]
            kw = jax.random.fold_in(ks[1], i)
            inp[f'W{i}'] = jax.random.normal(kw, (cout, cin), dtype=jnp.float32) / np.sqrt(cin)
            inp[f'b{i}'] = jnp.zeros((cout,), dtype=jnp.float32)
        return inp
    _L0_rec_all = _L0_rec_setup()
    _L0_rec_in = {k: v for k, v in _L0_rec_all.items() if k in ('W0', 'b0', 'W1', 'b1', 'W2', 'b2')}
    del _L0_rec_all
    return {'dense_ctx': dense_ctx, 'ids': ids, 'tbl_0': tbl_0, 'tbl_1': tbl_1, 'tbl_2': tbl_2, 'tbl_3': tbl_3, 'tbl_4': tbl_4, 'tbl_5': tbl_5, 'tbl_6': tbl_6, 'tbl_7': tbl_7, 'tbl_8': tbl_8, 'tbl_9': tbl_9, 'tbl_10': tbl_10, 'tbl_11': tbl_11, 'tbl_12': tbl_12, 'tbl_13': tbl_13, 'tbl_14': tbl_14, 'tbl_15': tbl_15, 'tbl_16': tbl_16, 'tbl_17': tbl_17, 'tbl_18': tbl_18, 'tbl_19': tbl_19, 'tbl_20': tbl_20, 'tbl_21': tbl_21, 'tbl_22': tbl_22, 'tbl_23': tbl_23, 'tbl_24': tbl_24, 'tbl_25': tbl_25, 'tbl_26': tbl_26, 'tbl_27': tbl_27, 'tbl_28': tbl_28, 'tbl_29': tbl_29, 'tbl_30': tbl_30, 'tbl_31': tbl_31, 'tbl_32': tbl_32, 'tbl_33': tbl_33, 'tbl_34': tbl_34, 'tbl_35': tbl_35, 'tbl_36': tbl_36, 'tbl_37': tbl_37, 'tbl_38': tbl_38, 'W_top1': W_top1, 'b_top1': b_top1, 'W_top2': W_top2, 'b_top2': b_top2, 'W_top3': W_top3, 'L0_rec_W0': _L0_rec_in['W0'], 'L0_rec_b0': _L0_rec_in['b0'], 'L0_rec_W1': _L0_rec_in['W1'], 'L0_rec_b1': _L0_rec_in['b1'], 'L0_rec_W2': _L0_rec_in['W2'], 'L0_rec_b2': _L0_rec_in['b2']}

def reference(dense_ctx, ids, tbl_0, tbl_1, tbl_2, tbl_3, tbl_4, tbl_5, tbl_6, tbl_7, tbl_8, tbl_9, tbl_10, tbl_11, tbl_12, tbl_13, tbl_14, tbl_15, tbl_16, tbl_17, tbl_18, tbl_19, tbl_20, tbl_21, tbl_22, tbl_23, tbl_24, tbl_25, tbl_26, tbl_27, tbl_28, tbl_29, tbl_30, tbl_31, tbl_32, tbl_33, tbl_34, tbl_35, tbl_36, tbl_37, tbl_38, W_top1, b_top1, W_top2, b_top2, W_top3, L0_rec_W0, L0_rec_b0, L0_rec_W1, L0_rec_b1, L0_rec_W2, L0_rec_b2):
    import jax
    import jax.numpy as jnp

    def _L0_rec_ref(embedded_features, W0, b0, W1, b1, W2, b2):
        import jax, jax.numpy as jnp
        import numpy as np
        B, F0, D = (512, 39, 16)
        CIN = [128, 128, 128]

        def _cin_layer(X0, Xi, W, b):
            H = W.shape[0]
            F0_, Fi = (X0.shape[1], Xi.shape[1])
            Wr = W.reshape(H, F0_, Fi)
            return jnp.einsum('hjk,bjd,bkd->bhd', Wr, X0, Xi) + b[None, :, None]
        X0 = embedded_features
        Ws = [(W0, b0), (W1, b1), (W2, b2)]
        Xi = X0
        res = []
        for W, b in Ws:
            Xi = _cin_layer(X0, Xi, W, b)
            res.append(Xi.sum(axis=2))
        return jnp.concatenate(res, axis=1)
    e = jnp.stack([tbl_0[ids[:, 0]], tbl_1[ids[:, 1]], tbl_2[ids[:, 2]], tbl_3[ids[:, 3]], tbl_4[ids[:, 4]], tbl_5[ids[:, 5]], tbl_6[ids[:, 6]], tbl_7[ids[:, 7]], tbl_8[ids[:, 8]], tbl_9[ids[:, 9]], tbl_10[ids[:, 10]], tbl_11[ids[:, 11]], tbl_12[ids[:, 12]], tbl_13[ids[:, 13]], tbl_14[ids[:, 14]], tbl_15[ids[:, 15]], tbl_16[ids[:, 16]], tbl_17[ids[:, 17]], tbl_18[ids[:, 18]], tbl_19[ids[:, 19]], tbl_20[ids[:, 20]], tbl_21[ids[:, 21]], tbl_22[ids[:, 22]], tbl_23[ids[:, 23]], tbl_24[ids[:, 24]], tbl_25[ids[:, 25]], tbl_26[ids[:, 26]], tbl_27[ids[:, 27]], tbl_28[ids[:, 28]], tbl_29[ids[:, 29]], tbl_30[ids[:, 30]], tbl_31[ids[:, 31]], tbl_32[ids[:, 32]], tbl_33[ids[:, 33]], tbl_34[ids[:, 34]], tbl_35[ids[:, 35]], tbl_36[ids[:, 36]], tbl_37[ids[:, 37]], tbl_38[ids[:, 38]]], axis=1)
    z = _L0_rec_ref(e, L0_rec_W0, L0_rec_b0, L0_rec_W1, L0_rec_b1, L0_rec_W2, L0_rec_b2)
    z = z.reshape(z.shape[0], -1)
    h = jnp.concatenate([z, dense_ctx], axis=1)
    h = jnp.maximum(h @ W_top1 + b_top1, 0.0)
    h = jnp.maximum(h @ W_top2 + b_top2, 0.0)
    y = h @ W_top3
    return y

_drawn_inputs = setup_inputs


def setup_inputs(seed=0):
    import zlib

    import numpy as np

    out = dict(_drawn_inputs(seed))
    spreads = {'b_top1': (0.0, 0.1),
     'b_top2': (0.0, 0.1),
     'L0_rec_b0': (0.0, 0.1),
     'L0_rec_b1': (0.0, 0.1),
     'L0_rec_b2': (0.0, 0.1)}
    factors = {'tbl_0': 8.0,
     'tbl_1': 6.075,
     'tbl_2': 5.1,
     'tbl_3': 6.831,
     'tbl_4': 8.0,
     'tbl_5': 8.0,
     'tbl_6': 8.0,
     'tbl_7': 6.927,
     'tbl_8': 8.0,
     'tbl_9': 8.0,
     'tbl_10': 8.0,
     'tbl_11': 6.592,
     'tbl_12': 8.0,
     'tbl_13': 8.0,
     'tbl_14': 4.221,
     'tbl_15': 5.579,
     'tbl_16': 8.0,
     'tbl_17': 8.0,
     'tbl_18': 8.0,
     'tbl_19': 6.178,
     'tbl_20': 7.348,
     'tbl_21': 8.0,
     'tbl_22': 8.0,
     'tbl_23': 8.0,
     'tbl_24': 8.0,
     'tbl_25': 7.241,
     'tbl_26': 5.867,
     'tbl_27': 8.0,
     'tbl_28': 8.0,
     'tbl_29': 8.0,
     'tbl_30': 6.525,
     'tbl_31': 6.621,
     'tbl_32': 8.0,
     'tbl_33': 7.391,
     'tbl_34': 8.0,
     'tbl_35': 6.407,
     'tbl_36': 7.873,
     'tbl_37': 6.567,
     'tbl_38': 8.0,
     'L0_rec_W0': 3.29}
    for name, (base, spread) in spreads.items():
        noise = np.random.default_rng([zlib.crc32(name.encode()), seed]).standard_normal(out[name].shape)
        drawn = base * np.exp(spread * noise) if base else spread * noise
        out[name] = jnp.asarray(drawn.astype(out[name].dtype))
    for name, factor in factors.items():
        out[name] = (out[name] * factor).astype(out[name].dtype)
    return out
```

```python
from contextlib import ExitStack

import numpy as np

import concourse.bass as bass
from concourse import mybir

F32 = mybir.dt.float32
I32 = mybir.dt.int32
ALU = mybir.AluOpType
ACT = mybir.ActivationFunctionType
AX_X = mybir.AxisListType.X

VOCABS = [12500, 12500, 1000, 1250, 1250, 1000, 1250, 125000, 125000, 1000, 125000, 125000, 1250,
          125000, 1250, 1000, 1250, 12500, 1000, 12500, 125000, 1250, 1250, 12500, 1000, 1000, 12500,
          1250, 12500, 125000, 125000, 12500, 125000, 125000, 1250, 12500, 12500, 1250, 1000]
B, FIELDS, D, H = 512, 39, 16, 128
CTX = 16
N1, N2 = 512, 256
COLS = B * D
CW = 512
CHUNKS = COLS // CW
CB = CW // D
HALF_CHUNKS = CHUNKS // 2
HB = B // 2
BLK_B = 128 // D
BLKS = CW // 128
SHIFTS = FIELDS // 2 + 1
SPT = 128 // FIELDS
PK = SPT * FIELDS
QT = -(-SHIFTS // SPT)
QT_LAST = (SHIFTS - (QT - 1) * SPT) * FIELDS
X_ROWS = SPT * QT - 1 + FIELDS
DUP = X_ROWS - FIELDS
GT = 4
L0_TILES = [GT, QT - GT]
L1_TILES = [GT] * (FIELDS // GT) + [FIELDS % GT]
L0G, L1G = len(L0_TILES), len(L1_TILES)
PER_CHUNK = L0G + L1G
XS, PS = 4, 3
FPG = 128 // CB
GATHERS = -(-FIELDS // FPG)
DUP_G = DUP // FPG


def needed(count):
    return not isinstance(count, int) or count > 0


def first_tile(k):
    return k * GT


def l0_index(m, k):
    return k if isinstance(m, int) and m == 0 else L0G + PER_CHUNK * (m - 1) + k


def l1_index(n, k, last):
    return L0G + PER_CHUNK * n + (0 if last else L0G) + k


def slot_of(kind, k, last, ring):
    index = L0G + k if kind == 0 else L0G + L0G + k
    if kind == 1 and last:
        index = L0G + PER_CHUNK * (CHUNKS - 1) + k
    return index % ring


def l1_loads_before(n, k, last):
    slot = slot_of(1, k, last, XS)
    regular = sum(slot_of(1, i, False, XS) == slot for i in range(L1G))
    own = sum(slot_of(1, i, last, XS) == slot for i in range(k + 1))
    return n * regular + own


assert PER_CHUNK % XS == 0 and PER_CHUNK % PS == 0 and L0G == 2 and CHUNKS % 2 == 0


def build(nc, ids, bases, tables, x_rows, w0a, w0b, w1, w2, biases, ctx_in, wt1, wt1c, bt1, wt2, bt2, wt3,
          ident_in, mask_in, out):
    with ExitStack() as stack:
        def sb(name, shape, dt=F32):
            return stack.enter_context(nc.sbuf_tensor(name, shape, dt))

        def ps(name):
            return stack.enter_context(nc.psum_tensor(name, [128, 512], F32))

        def sem(name):
            return stack.enter_context(nc.semaphore(name))

        ids_sb = sb("ids_sb", [128, CHUNKS, GATHERS], I32)
        bases_sb = sb("bases_sb", [128, GATHERS], I32)
        index = sb("index", [128, CHUNKS, GATHERS], I32)
        rows_now = sb("rows_now", [128, 2, GATHERS], I32)
        passed = sb("passed", [128, 1], I32)
        emb = sb("emb", [128, 2, GATHERS, D])
        w0_sb = sb("w0_sb", [PK, QT, H])
        w0b_sb = sb("w0b_sb", [PK, QT, H])
        w1_sb = sb("w1_sb", [128, FIELDS, H])
        w2_sb = sb("w2_sb", [128, FIELDS, H])
        bias_sb = sb("bias_sb", [128, 3])
        bias2d = sb("bias2d", [128, 1])
        wt1_sb = sb("wt1_sb", [128, 3, N1])
        wt1c_sb = sb("wt1c_sb", [CTX, N1])
        bt1_sb = sb("bt1_sb", [128, N1 // 128])
        wt2_sb = sb("wt2_sb", [128, N1 // 128, N2])
        bt2_sb = sb("bt2_sb", [128, N2 // 128])
        wt3_sb = sb("wt3_sb", [128, N2 // 128])
        ctx_sb = sb("ctx_sb", [CTX, B])
        ident = sb("ident", [128, 128])
        mask = sb("mask", [128, BLK_B])
        factors = sb("factors", [128, XS, GT, CW])
        products = sb("products", [128, PS, GT, CW])
        rows3 = sb("rows3", [PK, CW])
        xrow = sb("xrow", [FIELDS, CW])
        x1 = sb("x1", [128, CW])
        x2 = sb("x2", [128, CW])
        x2t = sb("x2t", [128, BLKS, 128])
        diag = sb("diag", [128, BLKS, FIELDS, BLK_B])
        g_sb = sb("g_sb", [128, FIELDS, HB])
        z = sb("z", [128, 3, B])
        h1 = factors[:, 0, :, :]
        h2 = factors[:, 1, 0:N2 // 128, :]
        y_sb = sb("y_sb", [1, B])

        quad_ps, cubic_ps, xt_ps, x2t_ps = ps("quad_ps"), ps("cubic_ps"), ps("xt_ps"), ps("x2t_ps")
        g_ps = [ps("g_ps0"), ps("g_ps1")]
        z3_ps, y_ps = ps("z3_ps"), ps("y_ps")

        ids_loaded, index_ready = sem("ids_loaded"), sem("index_ready")
        rows_picked = sem("rows_picked")
        gathered, xd_written = sem("gathered"), sem("xd_written")
        w0_loaded, w1_loaded, late_loaded, small_loaded = (
            sem("w0_loaded"), sem("w1_loaded"), sem("late_loaded"), sem("small_loaded"))
        w0_ready, bias_ready = sem("w0_ready"), sem("bias_ready")
        shift_loaded = [sem(f"shift_loaded{i}") for i in range(XS)]
        xb_loaded = [sem(f"xb_loaded{i}") for i in range(XS)]
        rows3_loaded, xrow_loaded = sem("rows3_loaded"), sem("xrow_loaded")
        products_ready, groups_done = sem("products_ready"), sem("groups_done")
        quad_ready, x1_stored = sem("quad_ready"), sem("x1_stored")
        cubic_ready, x2_stored = sem("cubic_ready"), sem("x2_stored")
        xt_ready, diag_built = sem("xt_ready"), sem("diag_built")
        x2t_ready, x2t_stored = sem("x2t_ready"), sem("x2t_stored")
        g_ready, g_stored = sem("g_ready"), sem("g_stored")
        z1_summed, z2_summed = sem("z1_summed"), sem("z2_summed")
        z3_ready, z3_stored = sem("z3_ready"), sem("z3_stored")
        mlp_ready, mlp_stored = sem("mlp_ready"), sem("mlp_stored")
        out_written = sem("out_written")

        block = stack.enter_context(nc.Block())

        @block.gpsimd
        def _(pool):
            pool.wait_ge(ids_loaded, 32)
            for m in range(CHUNKS):
                last = nc.gpsimd.tensor_tensor(index[:, m, :], ids_sb[:, m, :], bases_sb[:, :], ALU.add)
            last.then_inc(index_ready, 1)
            pool.wait_ge(index_ready, 1)

            def gather(m, buf):
                nc.gpsimd.tensor_copy(rows_now[:, buf, :], index[:, m, :] if isinstance(m, int)
                                      else index[:, bass.ds(m, 1), :].rearrange("p a g -> p (a g)")
                                      ).then_inc(rows_picked, 1)
                pool.wait_ge(rows_picked, m + 1)
                nc.gpsimd.tensor_tensor(passed[:, :], index[:, 0, 0:1], index[:, 0, 0:1], ALU.add)
                for g in range(GATHERS):
                    parts = CB * min(FPG, FIELDS - g * FPG)
                    nc.gpsimd.indirect_dma_start(
                        out=emb[0:parts, buf, g, :], out_offset=None, in_=tables[:, :],
                        in_offset=bass.IndirectOffsetOnAxis(ap=rows_now[0:parts, buf, g:g + 1], axis=0),
                    ).then_inc(gathered, 16)
                pool.wait_ge(gathered, 16 * GATHERS * (m + 1))

            gather(0, 0)
            gather(1, 1)
            with pool.Fori(2, CHUNKS) as m:
                pool.wait_ge(xd_written, 16 * 2 * FPG * m)
                gather(m, 1)

        @block.sync
        def _(sp):
            def write_x(m, buf):
                sp.wait_ge(gathered, 16 * GATHERS * (m + 1))
                for f in range(FPG):
                    full = GATHERS - 1 + (f < FIELDS - FPG * (GATHERS - 1))
                    src = emb[CB * f:CB * (f + 1), buf, 0:full, :]
                    for row, count in ((f, full), (FIELDS + f, DUP_G)):
                        dst = x_rows[row:row + FPG * (count - 1) + 1:FPG, bass.ds(m * CW, CW)]
                        sp.dma_start(dst.rearrange("g (b d) -> b g d", d=D), src[:, 0:count, :]
                                     ).then_inc(xd_written, 16)

            def load_l0(m):
                sp.wait_ge(xd_written, 16 * 2 * FPG * (m + 1))
                if not (isinstance(m, int) and m == 0):
                    sp.wait_ge(products_ready, l0_index(m - 1, L0G - 1) + 1)
                for s in range(SPT):
                    sp.dma_start(rows3[FIELDS * s:FIELDS * (s + 1), :], x_rows[0:FIELDS, bass.ds(m * CW, CW)]
                                 ).then_inc(rows3_loaded, 16)
                for k, tiles in enumerate(L0_TILES):
                    slot = slot_of(0, k, False, XS) if not (isinstance(m, int) and m == 0) else k
                    if needed(l0_index(m, k) - XS + 1):
                        sp.wait_ge(products_ready, l0_index(m, k) - XS + 1)
                    for s in range(SPT):
                        row = SPT * first_tile(k) + s
                        for t in range(tiles):
                            sp.dma_start(factors[FIELDS * s:FIELDS * (s + 1), slot, t, :],
                                         x_rows[row + SPT * t:row + SPT * t + FIELDS, bass.ds(m * CW, CW)]
                                         ).then_inc(shift_loaded[slot], 16)

            def load_l1(n, last):
                for k, tiles in enumerate(L1_TILES):
                    slot = slot_of(1, k, last, XS)
                    if needed(l1_index(n, k, last) - XS + 1):
                        sp.wait_ge(products_ready, l1_index(n, k, last) - XS + 1)
                    j = first_tile(k)
                    src = x_rows[j:j + tiles, bass.ds(n * CW, CW)].partition_broadcast(128)
                    sp.dma_start(factors[:, slot, 0:tiles, :], src).then_inc(xb_loaded[slot], 16)

            def load_xrow(c):
                if not (isinstance(c, int) and c == 0):
                    sp.wait_ge(groups_done, l1_index(c, 0, False) + 1)
                sp.dma_start(xrow[:, :], x_rows[0:FIELDS, bass.ds(c * CW, CW)]).then_inc(xrow_loaded, 16)

            sp.dma_start(ids_sb[:, :, :], ids).then_inc(ids_loaded, 16)
            sp.dma_start(bases_sb[:, :], bases).then_inc(ids_loaded, 16)
            sp.dma_start(w0_sb[:, :, :], w0a).then_inc(w0_loaded, 16)
            sp.dma_start(w0b_sb[:, :, :], w0b).then_inc(w0_loaded, 16)
            sp.dma_start(bias_sb[:, :], biases).then_inc(small_loaded, 16)
            sp.dma_start(ident[:, :], ident_in).then_inc(small_loaded, 16)
            sp.dma_start(mask[:, :], mask_in).then_inc(small_loaded, 16)
            sp.dma_start(w1_sb[:, :, :], w1).then_inc(w1_loaded, 16)
            write_x(0, 0)
            load_l0(0)
            write_x(1, 1)

            def body(n, first=False, last=False):
                if not last:
                    load_l0(n + 1)
                if first:
                    for dst, src in ((w2_sb, w2), (wt1_sb, wt1), (wt1c_sb, wt1c), (bt1_sb, bt1), (wt2_sb, wt2),
                                     (bt2_sb, bt2), (wt3_sb, wt3), (ctx_sb, ctx_in)):
                        sp.dma_start(dst[tuple([slice(None)] * len(dst.shape))], src).then_inc(late_loaded, 16)
                else:
                    load_xrow(n - 1)
                load_l1(n, last)

            body(0, first=True)
            write_x(2, 1)
            with sp.Fori(1, HALF_CHUNKS) as n:
                body(n)
                write_x(n + 2, 1)
            body(HALF_CHUNKS)
            write_x(HALF_CHUNKS + 2, 1)
            with sp.Fori(HALF_CHUNKS + 1, CHUNKS - 2) as n:
                body(n)
                write_x(n + 2, 1)
            body(CHUNKS - 2)
            body(CHUNKS - 1, last=True)
            load_xrow(CHUNKS - 1)
            sp.wait_ge(mlp_stored, N1 // 128 + N2 // 128 + 1)
            sp.dma_start(out, y_sb[:, :]).then_inc(out_written, 16)
            sp.wait_ge(out_written, 16)

        @block.vector
        def _(dve):
            dve.wait_ge(w0_loaded, 32)
            nc.vector.tensor_tensor(w0_sb[:, :, :], w0_sb[:, :, :], w0b_sb[:, :, :], ALU.add
                                    ).then_inc(w0_ready, 1)
            dve.wait_ge(small_loaded, 48)
            nc.vector.tensor_scalar(bias2d[:, :], bias_sb[:, 2:3], float(D), None, ALU.mult
                                    ).then_inc(bias_ready, 1)

            def multiply_l0(m):
                start = isinstance(m, int) and m == 0
                dve.wait_ge(rows3_loaded, 16 * SPT * (m + 1))
                for k, tiles in enumerate(L0_TILES):
                    index = l0_index(m, k)
                    xs, pslot = (k, k) if start else (slot_of(0, k, False, XS), slot_of(0, k, False, PS))
                    if needed(index - PS + 1):
                        dve.wait_ge(groups_done, index - PS + 1)
                    dve.wait_ge(shift_loaded[xs], 16 * SPT * tiles * ((m + 1) if start else m))
                    nc.vector.tensor_tensor(
                        products[0:PK, pslot, 0:tiles, :], factors[0:PK, xs, 0:tiles, :],
                        rows3[:, None, :].to_broadcast([PK, tiles, CW]), ALU.mult).then_inc(products_ready, 1)

            def multiply_l1(n, last, k):
                index = l1_index(n, k, last)
                xs, pslot = slot_of(1, k, last, XS), slot_of(1, k, last, PS)
                tiles = L1_TILES[k]
                dve.wait_ge(xb_loaded[xs], 16 * l1_loads_before(n, k, last))
                dve.wait_ge(groups_done, index - PS + 1)
                nc.vector.tensor_tensor(
                    products[:, pslot, 0:tiles, :], factors[:, xs, 0:tiles, :],
                    x1[:, None, :].to_broadcast([128, tiles, CW]), ALU.mult).then_inc(products_ready, 1)

            def sum_d(z_row, c, src, signal):
                nc.vector.tensor_reduce(z[:, z_row, bass.ds(c * CB, CB)], src.rearrange("p (b d) -> p b d", d=D),
                                        AX_X, ALU.add).then_inc(signal, 1)

            def sum_x2(c):
                dve.wait_ge(x2_stored, c + 1)
                sum_d(1, c, x2[:, :], z2_summed)

            def body(n, first=False, last=False):
                if not last:
                    multiply_l0(n + 1)
                if not first:
                    sum_x2(n - 1)
                dve.wait_ge(x1_stored, n + 1)
                for k in range(L1G):
                    multiply_l1(n, last, k)
                    if k == 2:
                        sum_d(0, n, x1[:, :], z1_summed)

            multiply_l0(0)
            body(0, first=True)
            with dve.Fori(1, HALF_CHUNKS) as n:
                body(n)
            body(HALF_CHUNKS)
            with dve.Fori(HALF_CHUNKS + 1, CHUNKS - 1) as n:
                body(n)
            body(CHUNKS - 1, last=True)
            sum_x2(CHUNKS - 1)

        @block.tensor
        def _(pe):
            def layer0(m):
                start = isinstance(m, int) and m == 0
                if start:
                    pe.wait_ge(w0_ready, 1)
                else:
                    pe.wait_ge(x1_stored, m)
                for k, tiles in enumerate(L0_TILES):
                    pslot = k if start else slot_of(0, k, False, PS)
                    pe.wait_ge(products_ready, l0_index(m, k) + 1)
                    for t in range(tiles):
                        tile = first_tile(k) + t
                        parts = PK if tile < QT - 1 else QT_LAST
                        mm = nc.tensor.matmul(quad_ps[:, :], w0_sb[0:parts, tile, :],
                                              products[0:parts, pslot, t, :],
                                              start=(tile == 0), stop=(tile == QT - 1))
                        if t == tiles - 1 and k == 0:
                            mm.then_inc(groups_done, 1)
                mm.then_inc(groups_done, 1)

            def layer1(n, last, k):
                pslot = slot_of(1, k, last, PS)
                pe.wait_ge(products_ready, l1_index(n, k, last) + 1)
                for t in range(L1_TILES[k]):
                    j = first_tile(k) + t
                    mm = nc.tensor.matmul(cubic_ps[:, :], w1_sb[:, j, :], products[:, pslot, t, :],
                                          start=(j == 0), stop=(j == FIELDS - 1))
                mm.then_inc(groups_done, 1)

            def transposes(c):
                pe.wait_ge(xrow_loaded, 16 * (c + 1))
                pe.wait_ge(x2_stored, c + 1)
                for i in range(BLKS):
                    mm = nc.tensor.transpose(x2t_ps[:, 128 * i:128 * (i + 1)],
                                             x2[:, 128 * i:128 * (i + 1)], ident[:, :])
                mm.then_inc(x2t_ready, 1)
                for i in range(BLKS):
                    mm = nc.tensor.transpose(xt_ps[:, FIELDS * i:FIELDS * (i + 1)],
                                             xrow[:, 128 * i:128 * (i + 1)], ident[0:FIELDS, 0:FIELDS])
                mm.then_inc(xt_ready, 1)

            def g_block(c, i):
                if i == 0:
                    pe.wait_ge(diag_built, c + 1)
                    pe.wait_ge(x2t_stored, c + 1)
                if i >= 2:
                    pe.wait_ge(g_stored, BLKS * c + i - 1)
                nc.tensor.matmul(g_ps[i % 2][:, 0:FIELDS * BLK_B], x2t[:, i, :],
                                 diag[:, i, :, :].rearrange("p j b -> p (j b)"),
                                 start=True, stop=True).then_inc(g_ready, 1)

            def layer2(half):
                pe.wait_ge(g_stored, BLKS * HALF_CHUNKS * (half + 1))
                for j in range(FIELDS):
                    mm = nc.tensor.matmul(z3_ps[:, 0:HB], w2_sb[:, j, :], g_sb[:, j, :],
                                          start=(j == 0), stop=(j == FIELDS - 1))
                mm.then_inc(z3_ready, 1)

            def body(n, first=False, last=False, then=None):
                if not last:
                    layer0(n + 1)
                if not first:
                    transposes(n - 1)
                else:
                    pe.wait_ge(w1_loaded, 16)
                for k in range(L1G):
                    if k == 0 and not first:
                        pe.wait_ge(x2_stored, n)
                    layer1(n, last, k)
                    if not first and 2 <= k < 2 + BLKS:
                        g_block(n - 1, k - 2)
                    if k == 8 and then is not None:
                        then()

            pe.wait_ge(small_loaded, 48)
            layer0(0)
            body(0, first=True)
            with pe.Fori(1, HALF_CHUNKS) as n:
                body(n)
            pe.wait_ge(late_loaded, 16 * 8)
            body(HALF_CHUNKS, then=lambda: layer2(0))
            with pe.Fori(HALF_CHUNKS + 1, CHUNKS - 1) as n:
                body(n)
            body(CHUNKS - 1, last=True)
            transposes(CHUNKS - 1)
            for i in range(BLKS):
                g_block(CHUNKS - 1, i)
            layer2(1)

            banks = [quad_ps, cubic_ps, xt_ps, x2t_ps]
            pe.wait_ge(z1_summed, CHUNKS)
            pe.wait_ge(z2_summed, CHUNKS)
            for mt in range(N1 // 128):
                cols = slice(128 * mt, 128 * (mt + 1))
                nc.tensor.matmul(banks[mt][:, :], wt1_sb[:, 0, cols], z[:, 0, :], start=True, stop=False)
                nc.tensor.matmul(banks[mt][:, :], wt1_sb[:, 1, cols], z[:, 1, :], start=False, stop=False)
                nc.tensor.matmul(banks[mt][:, :], wt1c_sb[:, cols], ctx_sb[:, :], start=False, stop=False)
            pe.wait_ge(z3_stored, 2)
            for mt in range(N1 // 128):
                nc.tensor.matmul(banks[mt][:, :], wt1_sb[:, 2, 128 * mt:128 * (mt + 1)], z[:, 2, :],
                                 start=False, stop=True).then_inc(mlp_ready, 1)
            for mt in range(N2 // 128):
                for kt in range(N1 // 128):
                    if mt == 0:
                        pe.wait_ge(mlp_stored, kt + 1)
                    mm = nc.tensor.matmul(g_ps[mt][:, :], wt2_sb[:, kt, 128 * mt:128 * (mt + 1)], h1[:, kt, :],
                                          start=(kt == 0), stop=(kt == N1 // 128 - 1))
                mm.then_inc(mlp_ready, 1)
            for kt in range(N2 // 128):
                pe.wait_ge(mlp_stored, N1 // 128 + kt + 1)
                mm = nc.tensor.matmul(y_ps[0:1, :], wt3_sb[:, kt:kt + 1], h2[:, kt, :],
                                      start=(kt == 0), stop=(kt == N2 // 128 - 1))
            mm.then_inc(mlp_ready, 1)

        @block.scalar
        def _(act):
            def store_x1(m):
                if not (isinstance(m, int) and m == 0):
                    act.wait_ge(products_ready, l1_index(m - 1, L1G - 1, False) + 1)
                    act.wait_ge(z1_summed, m)
                act.wait_ge(groups_done, l0_index(m, L0G - 1) + 1)
                nc.scalar.activation(x1[:, :], quad_ps[:, :], ACT.Identity, bias=bias_sb[:, 0:1]
                                     ).then_inc(x1_stored, 1)

            def store_x2(c, last=False):
                act.wait_ge(groups_done, l1_index(c, L1G - 1, last) + 1)
                nc.scalar.activation(x2[:, :], cubic_ps[:, :], ACT.Identity, bias=bias_sb[:, 1:2]
                                     ).then_inc(x2_stored, 1)

            def build_diag(c):
                act.wait_ge(xt_ready, c + 1)
                src = xt_ps[:, 0:BLKS * FIELDS].rearrange("p (i j) -> p i j", j=FIELDS)
                for b in range(BLK_B):
                    last = nc.scalar.activation(diag[:, :, :, b], src, ACT.Copy, scale=mask[:, b:b + 1])
                last.then_inc(diag_built, 1)
                act.wait_ge(x2t_ready, c + 1)
                nc.scalar.copy(x2t[:, :, :], x2t_ps[:, :].rearrange("p (i k) -> p i k", k=128)
                               ).then_inc(x2t_stored, 1)

            def store_g(c, half, i):
                act.wait_ge(g_ready, BLKS * c + i + 1)
                nc.scalar.copy(g_sb[:, :, bass.ds(c * CB + (i * BLK_B - half * HB), BLK_B)],
                               g_ps[i % 2][:, 0:FIELDS * BLK_B].rearrange("p (j b) -> p j b", b=BLK_B)
                               ).then_inc(g_stored, 1)

            def store_z3(half):
                act.wait_ge(z3_ready, half + 1)
                nc.scalar.activation(z[:, 2, HB * half:HB * (half + 1)], z3_ps[:, 0:HB], ACT.Identity,
                                     bias=bias2d[:, :]).then_inc(z3_stored, 1)

            def body(n, half, first=False, last=False):
                if not first:
                    store_x2(n - 1)
                    build_diag(n - 1)
                    for i in range(BLKS):
                        store_g(n - 1, half, i)
                if not last:
                    store_x1(n + 1)

            act.wait_ge(small_loaded, 48)
            act.wait_ge(bias_ready, 1)
            store_x1(0)
            body(0, 0, first=True)
            with act.Fori(1, HALF_CHUNKS) as n:
                body(n, 0)
            body(HALF_CHUNKS, 0)
            store_z3(0)
            with act.Fori(HALF_CHUNKS + 1, CHUNKS - 1) as n:
                body(n, 1)
            body(CHUNKS - 1, 1, last=True)
            store_x2(CHUNKS - 1, last=True)
            build_diag(CHUNKS - 1)
            for i in range(BLKS):
                store_g(CHUNKS - 1, 1, i)
            store_z3(1)
            banks = [quad_ps, cubic_ps, xt_ps, x2t_ps]
            for mt in range(N1 // 128):
                act.wait_ge(mlp_ready, mt + 1)
                nc.scalar.activation(h1[:, mt, :], banks[mt][:, :], ACT.Relu, bias=bt1_sb[:, mt:mt + 1]
                                     ).then_inc(mlp_stored, 1)
            for mt in range(N2 // 128):
                act.wait_ge(mlp_ready, N1 // 128 + mt + 1)
                nc.scalar.activation(h2[:, mt, :], g_ps[mt][:, :], ACT.Relu, bias=bt2_sb[:, mt:mt + 1]
                                     ).then_inc(mlp_stored, 1)
            act.wait_ge(mlp_ready, N1 // 128 + N2 // 128 + 1)
            nc.scalar.copy(y_sb[:, :], y_ps[0:1, :]).then_inc(mlp_stored, 1)


def kernel(**inputs):
    import concourse.bacc as bacc
    from concourse.bass_utils import run_bass_kernel_spmd

    a = {k: np.asarray(v) for k, v in inputs.items()}
    ids = np.zeros((GATHERS * FPG, B), np.int32)
    ids[:FIELDS] = a["ids"].T
    ids = ids.reshape(GATHERS, FPG, CHUNKS, CB).transpose(1, 3, 2, 0).reshape(128, CHUNKS, GATHERS)
    first = np.zeros(GATHERS * FPG, np.int32)
    first[:FIELDS] = np.concatenate([[0], np.cumsum(VOCABS)[:-1]])
    bases = np.repeat(first.reshape(GATHERS, FPG).T, CB, axis=0)
    tables = np.concatenate([a[f"tbl_{f}"] for f in range(FIELDS)], axis=0)
    w0 = a["L0_rec_W0"].reshape(H, FIELDS, FIELDS)
    j = np.arange(FIELDS)[None, :, None]
    s = np.arange(SPT)[:, None, None] + SPT * np.arange(QT)[None, None, :]
    k = (j + s) % FIELDS
    j = np.broadcast_to(j, k.shape)
    w0a = w0[:, j, k].transpose(1, 2, 3, 0).reshape(PK, QT, H)
    w0b = w0[:, k, j].transpose(1, 2, 3, 0).reshape(PK, QT, H).copy()
    w0b[:FIELDS, 0] = 0
    by_j = lambda w: w.reshape(H, FIELDS, H).transpose(2, 1, 0)
    mask = (np.arange(128)[:, None] // D == np.arange(BLK_B)[None, :]).astype(np.float32)
    arrays = {
        "ids": ids, "bases": bases, "tables": tables, "w0a": w0a, "w0b": w0b,
        "w1": by_j(a["L0_rec_W1"]), "w2": by_j(a["L0_rec_W2"]),
        "biases": np.stack([a[f"L0_rec_b{i}"] for i in range(3)], axis=1),
        "ctx_in": a["dense_ctx"].T,
        "wt1": a["W_top1"][:3 * 128].reshape(3, 128, N1).transpose(1, 0, 2), "wt1c": a["W_top1"][3 * 128:],
        "bt1": a["b_top1"].reshape(N1 // 128, 128).T,
        "wt2": a["W_top2"].reshape(N1 // 128, 128, N2).transpose(1, 0, 2),
        "bt2": a["b_top2"].reshape(N2 // 128, 128).T, "wt3": a["W_top3"].reshape(N2 // 128, 128).T,
        "ident_in": np.eye(128, dtype=np.float32), "mask_in": mask,
    }
    arrays = {f"{k}_dram": np.ascontiguousarray(v) for k, v in arrays.items()}
    nc = bacc.Bacc("TRN2", target_bir_lowering=False, num_devices=1)
    aps = {n.removesuffix("_dram"): nc.dram_tensor(n, v.shape, mybir.dt.from_np(v.dtype), kind="ExternalInput").ap()
           for n, v in arrays.items()}
    aps["x_rows"] = nc.dram_tensor("x_rows", (X_ROWS, COLS), F32, kind="Internal").ap()
    aps["out"] = nc.dram_tensor("out_dram", (1, B), F32, kind="ExternalOutput").ap()
    build(nc, **aps)
    r = run_bass_kernel_spmd(nc, [arrays], core_ids=[0])
    return r.results[0]["out_dram"].reshape(B, 1)
```

```python
from contextlib import ExitStack

import numpy as np

import concourse.bass as bass
from concourse import mybir

F32 = mybir.dt.float32
F32R = mybir.dt.float32r
I32 = mybir.dt.int32
ALU = mybir.AluOpType
ACT = mybir.ActivationFunctionType
AX_X = mybir.AxisListType.X

VOCABS = [12500, 12500, 1000, 1250, 1250, 1000, 1250, 125000, 125000, 1000, 125000, 125000, 1250,
          125000, 1250, 1000, 1250, 12500, 1000, 12500, 125000, 1250, 1250, 12500, 1000, 1000, 12500,
          1250, 12500, 125000, 125000, 12500, 125000, 125000, 1250, 12500, 12500, 1250, 1000]
B, FIELDS, D, H = 512, 39, 16, 128
CTX = 16
N1, N2 = 512, 256
COLS = B * D
CW = 512
CHUNKS = COLS // CW
CB = CW // D
HALF_CHUNKS = CHUNKS // 2
HB = B // 2
BLK_B = 128 // D
BLKS = CW // 128
SHIFTS = FIELDS // 2 + 1
SPT = 128 // FIELDS
PK = SPT * FIELDS
QT = -(-SHIFTS // SPT)
QT_LAST = (SHIFTS - (QT - 1) * SPT) * FIELDS
X_ROWS = SPT * QT - 1 + FIELDS
DUP = X_ROWS - FIELDS
GT = 4
L0_TILES = [GT, QT - GT]
L1_TILES = [GT] * (FIELDS // GT) + [FIELDS % GT]
L0G, L1G = len(L0_TILES), len(L1_TILES)
PER_CHUNK = L0G + L1G
XS, PS, HS = 4, 3, 2
SPLIT = 2
SPLIT_J = [j for j in range(FIELDS) if j % GT < SPLIT]
NATIVE_J = [j for j in range(FIELDS) if j % GT >= SPLIT]
FPG = 128 // CB
GATHERS = -(-FIELDS // FPG)
DUP_G = DUP // FPG


def needed(count):
    return not isinstance(count, int) or count > 0


def first_tile(k):
    return k * GT


def l0_index(m, k):
    return k if isinstance(m, int) and m == 0 else L0G + PER_CHUNK * (m - 1) + k


def l1_index(n, k, last):
    return L0G + PER_CHUNK * n + (0 if last else L0G) + k


def slot_of(kind, k, last, ring):
    index = L0G + k if kind == 0 else L0G + L0G + k
    if kind == 1 and last:
        index = L0G + PER_CHUNK * (CHUNKS - 1) + k
    return index % ring


def l1_loads_before(n, k, last):
    slot = slot_of(1, k, last, XS)
    regular = sum(slot_of(1, i, False, XS) == slot for i in range(L1G))
    own = sum(slot_of(1, i, last, XS) == slot for i in range(k + 1))
    return n * regular + own


assert L1G % HS == 0 and min(L1_TILES) >= SPLIT
assert PER_CHUNK % XS == 0 and PER_CHUNK % PS == 0 and L0G == 2 and CHUNKS % 2 == 0


def build(nc, ids, bases, tables, x_rows, w0a, w0b, w1n, w1s, w2, biases, ctx_in, wt1, wt1c, bt1, wt2, bt2, wt3,
          ident_in, mask_in, out):
    with ExitStack() as stack:
        def sb(name, shape, dt=F32):
            return stack.enter_context(nc.sbuf_tensor(name, shape, dt))

        def ps(name):
            return stack.enter_context(nc.psum_tensor(name, [128, 512], F32))

        def sem(name):
            return stack.enter_context(nc.semaphore(name))

        ids_sb = sb("ids_sb", [128, CHUNKS, GATHERS], I32)
        bases_sb = sb("bases_sb", [128, GATHERS], I32)
        index = sb("index", [128, CHUNKS, GATHERS], I32)
        rows_now = sb("rows_now", [128, 2, GATHERS], I32)
        passed = sb("passed", [128, 1], I32)
        emb = sb("emb", [128, 2, GATHERS, D])
        w0_sb = sb("w0_sb", [PK, QT, H])
        w1_sb = sb("w1_sb", [128, len(NATIVE_J), H])
        w1_hi = sb("w1_hi", [128, len(SPLIT_J), H], F32R)
        w1_lo = sb("w1_lo", [128, len(SPLIT_J), H], F32R)
        w2_sb = sb("w2_sb", [128, FIELDS, H])
        bias_sb = sb("bias_sb", [128, 3])
        bias2d = sb("bias2d", [128, 1])
        bt1_sb = sb("bt1_sb", [128, N1 // 128])
        bt2_sb = sb("bt2_sb", [128, N2 // 128])
        wt3_sb = sb("wt3_sb", [128, N2 // 128])
        ident = sb("ident", [128, 128])
        mask = sb("mask", [128, BLK_B])
        factors = sb("factors", [128, XS, GT, CW])
        products = sb("products", [128, PS, GT, CW])
        rows3 = sb("rows3", [PK, CW])
        xrow = sb("xrow", [FIELDS, CW])
        x1 = sb("x1", [128, CW])
        x2 = sb("x2", [128, CW])
        halves_hi = sb("halves_hi", [128, HS, SPLIT, CW], F32R)
        halves_lo = sb("halves_lo", [128, HS, SPLIT, CW], F32R)
        x2t_hi = sb("x2t_hi", [128, CW], F32R)
        x2t_lo = sb("x2t_lo", [128, CW], F32R)
        xt_hi = sb("xt_hi", [128, BLKS * FIELDS], F32R)
        xt_lo = sb("xt_lo", [128, BLKS * FIELDS])
        diag_hi = sb("diag_hi", [128, BLKS, FIELDS, BLK_B], F32R)
        diag_lo = sb("diag_lo", [128, BLKS, FIELDS, BLK_B], F32R)
        g_sb = sb("g_sb", [128, FIELDS, HB])
        z = sb("z", [128, 3, B])
        w0b_sb = g_sb[0:PK, 0:QT, 0:H]
        w1s_sb = g_sb[:, QT:QT + len(SPLIT_J), 0:H]
        h1 = factors[:, 0, :, :]
        h2 = factors[:, 1, 0:N2 // 128, :]
        y_sb = factors[0:1, 1, 2, :]
        ctx_sb = factors[0:CTX, 1, 3, :]
        wt1_sb = products[:, 0, 0:3, :]
        wt1c_sb = products[0:CTX, 0, 3, :]
        wt2_sb = products[:, 1, 0:N1 * N2 // 128 // CW, :].rearrange("p a (t n) -> p (a t) n", n=N2)

        quad_ps, cubic_ps, xt_ps, x2t_ps = ps("quad_ps"), ps("cubic_ps"), ps("xt_ps"), ps("x2t_ps")
        g_ps = [ps("g_ps0"), ps("g_ps1")]
        z3_ps, y_ps = ps("z3_ps"), ps("y_ps")

        ids_loaded, index_ready = sem("ids_loaded"), sem("index_ready")
        rows_picked = sem("rows_picked")
        gathered, xd_written = sem("gathered"), sem("xd_written")
        w0_loaded, w1_loaded, late_loaded, small_loaded = (
            sem("w0_loaded"), sem("w1_loaded"), sem("late_loaded"), sem("small_loaded"))
        w0_ready, bias_ready = sem("w0_ready"), sem("bias_ready")
        w1_hi_ready, w1_lo_ready = sem("w1_hi_ready"), sem("w1_lo_ready")
        hi_ready, lo_ready = sem("hi_ready"), sem("lo_ready")
        xt_hi_ready, xt_lo_ready = sem("xt_hi_ready"), sem("xt_lo_ready")
        x2t_hi_ready, x2t_lo_ready = sem("x2t_hi_ready"), sem("x2t_lo_ready")
        mlp_loaded = sem("mlp_loaded")
        shift_loaded = [sem(f"shift_loaded{i}") for i in range(XS)]
        xb_loaded = [sem(f"xb_loaded{i}") for i in range(XS)]
        rows3_loaded, xrow_loaded = sem("rows3_loaded"), sem("xrow_loaded")
        products_ready, groups_done = sem("products_ready"), sem("groups_done")
        quad_ready, x1_stored = sem("quad_ready"), sem("x1_stored")
        cubic_ready, x2_stored = sem("cubic_ready"), sem("x2_stored")
        xt_ready, diag_built = sem("xt_ready"), sem("diag_built")
        x2t_ready = sem("x2t_ready")
        g_ready, g_stored = sem("g_ready"), sem("g_stored")
        z1_summed, z2_summed = sem("z1_summed"), sem("z2_summed")
        z3_ready, z3_stored = sem("z3_ready"), sem("z3_stored")
        mlp_ready, mlp_stored = sem("mlp_ready"), sem("mlp_stored")
        out_written = sem("out_written")

        block = stack.enter_context(nc.Block())

        @block.gpsimd
        def _(pool):
            pool.wait_ge(ids_loaded, 32)
            for m in range(CHUNKS):
                last = nc.gpsimd.tensor_tensor(index[:, m, :], ids_sb[:, m, :], bases_sb[:, :], ALU.add)
            last.then_inc(index_ready, 1)
            pool.wait_ge(index_ready, 1)

            def gather(m, buf):
                nc.gpsimd.tensor_copy(rows_now[:, buf, :], index[:, m, :] if isinstance(m, int)
                                      else index[:, bass.ds(m, 1), :].rearrange("p a g -> p (a g)")
                                      ).then_inc(rows_picked, 1)
                pool.wait_ge(rows_picked, m + 1)
                nc.gpsimd.tensor_tensor(passed[:, :], index[:, 0, 0:1], index[:, 0, 0:1], ALU.add)
                for g in range(GATHERS):
                    parts = CB * min(FPG, FIELDS - g * FPG)
                    nc.gpsimd.indirect_dma_start(
                        out=emb[0:parts, buf, g, :], out_offset=None, in_=tables[:, :],
                        in_offset=bass.IndirectOffsetOnAxis(ap=rows_now[0:parts, buf, g:g + 1], axis=0),
                    ).then_inc(gathered, 16)
                pool.wait_ge(gathered, 16 * GATHERS * (m + 1))

            gather(0, 0)
            gather(1, 1)
            with pool.Fori(2, CHUNKS) as m:
                pool.wait_ge(xd_written, 16 * 2 * FPG * m)
                gather(m, 1)

        @block.sync
        def _(sp):
            def write_x(m, buf):
                sp.wait_ge(gathered, 16 * GATHERS * (m + 1))
                for f in range(FPG):
                    full = GATHERS - 1 + (f < FIELDS - FPG * (GATHERS - 1))
                    src = emb[CB * f:CB * (f + 1), buf, 0:full, :]
                    for row, count in ((f, full), (FIELDS + f, DUP_G)):
                        dst = x_rows[row:row + FPG * (count - 1) + 1:FPG, bass.ds(m * CW, CW)]
                        sp.dma_start(dst.rearrange("g (b d) -> b g d", d=D), src[:, 0:count, :]
                                     ).then_inc(xd_written, 16)

            def load_l0(m):
                sp.wait_ge(xd_written, 16 * 2 * FPG * (m + 1))
                if not (isinstance(m, int) and m == 0):
                    sp.wait_ge(products_ready, l0_index(m - 1, L0G - 1) + 1)
                for s in range(SPT):
                    sp.dma_start(rows3[FIELDS * s:FIELDS * (s + 1), :], x_rows[0:FIELDS, bass.ds(m * CW, CW)]
                                 ).then_inc(rows3_loaded, 16)
                for k, tiles in enumerate(L0_TILES):
                    slot = slot_of(0, k, False, XS) if not (isinstance(m, int) and m == 0) else k
                    if needed(l0_index(m, k) - XS + 1):
                        sp.wait_ge(products_ready, l0_index(m, k) - XS + 1)
                    for s in range(SPT):
                        src = bass.AP(x_rows.tensor, (SPT * first_tile(k) + s) * COLS + m * CW,
                                      [[COLS, FIELDS], [SPT * COLS, tiles], [1, CW]])
                        sp.dma_start(factors[FIELDS * s:FIELDS * (s + 1), slot, 0:tiles, :], src
                                     ).then_inc(shift_loaded[slot], 16)

            def load_l1(n, last, write=None):
                for k, tiles in enumerate(L1_TILES):
                    if k == L1G // 2 and write is not None:
                        write_x(*write)
                    slot = slot_of(1, k, last, XS)
                    if needed(l1_index(n, k, last) - XS + 1):
                        sp.wait_ge(products_ready, l1_index(n, k, last) - XS + 1)
                    j = first_tile(k)
                    src = x_rows[j:j + tiles, bass.ds(n * CW, CW)].partition_broadcast(128)
                    sp.dma_start(factors[:, slot, 0:tiles, :], src).then_inc(xb_loaded[slot], 16)

            def load_xrow(c):
                if not (isinstance(c, int) and c == 0):
                    sp.wait_ge(groups_done, l1_index(c, 0, False) + 1)
                sp.dma_start(xrow[:, :], x_rows[0:FIELDS, bass.ds(c * CW, CW)]).then_inc(xrow_loaded, 16)

            sp.dma_start(ids_sb[:, :, :], ids).then_inc(ids_loaded, 16)
            sp.dma_start(bases_sb[:, :], bases).then_inc(ids_loaded, 16)
            sp.dma_start(w0_sb[:, :, :], w0a).then_inc(w0_loaded, 16)
            sp.dma_start(w0b_sb[:, :, :], w0b).then_inc(w0_loaded, 16)
            sp.dma_start(bias_sb[:, :], biases).then_inc(small_loaded, 16)
            sp.dma_start(ident[:, :], ident_in).then_inc(small_loaded, 16)
            sp.dma_start(mask[:, :], mask_in).then_inc(small_loaded, 16)
            sp.dma_start(w1s_sb, w1s).then_inc(w1_loaded, 16)
            sp.dma_start(w1_sb[:, :, :], w1n).then_inc(w1_loaded, 16)
            write_x(0, 0)
            load_l0(0)
            write_x(1, 1)

            def body(n, first=False, last=False, write=True):
                if not last:
                    load_l0(n + 1)
                if first:
                    sp.dma_start(w2_sb[:, :, :], w2).then_inc(late_loaded, 16)
                    for dst, src in ((bt1_sb, bt1), (bt2_sb, bt2), (wt3_sb, wt3)):
                        sp.dma_start(dst[:, :], src).then_inc(late_loaded, 16)
                else:
                    load_xrow(n - 1)
                load_l1(n, last, (n + 2, 1) if write else None)

            body(0, first=True)
            with sp.Fori(1, CHUNKS - 2) as n:
                body(n)
            body(CHUNKS - 2, write=False)
            body(CHUNKS - 1, last=True, write=False)
            load_xrow(CHUNKS - 1)
            sp.wait_ge(groups_done, l1_index(CHUNKS - 1, L1G - 1, True) + 1)
            for dst, src in ((wt1_sb, wt1), (wt1c_sb, wt1c), (wt2_sb, wt2), (ctx_sb, ctx_in)):
                sp.dma_start(dst, src).then_inc(mlp_loaded, 16)
            sp.wait_ge(mlp_stored, N1 // 128 + N2 // 128 + 1)
            sp.dma_start(out, y_sb[:, :]).then_inc(out_written, 16)
            sp.wait_ge(out_written, 16)

        @block.vector
        def _(dve):
            dve.wait_ge(w0_loaded, 32)
            nc.vector.tensor_tensor(w0_sb[:, :, :], w0_sb[:, :, :], w0b_sb, ALU.add
                                    ).then_inc(w0_ready, 1)
            dve.wait_ge(small_loaded, 48)
            nc.vector.tensor_scalar(bias2d[:, :], bias_sb[:, 2:3], float(D), None, ALU.mult
                                    ).then_inc(bias_ready, 1)

            dve.wait_ge(w1_hi_ready, 1)
            nc.vector.tensor_tensor(w1_lo[:, :, :], w1s_sb, w1_hi[:, :, :].bitcast(F32), ALU.subtract
                                    ).then_inc(w1_lo_ready, 1)

            def multiply_l0(m):
                start = isinstance(m, int) and m == 0
                dve.wait_ge(rows3_loaded, 16 * SPT * (m + 1))
                for k, tiles in enumerate(L0_TILES):
                    index = l0_index(m, k)
                    xs, pslot = (k, k) if start else (slot_of(0, k, False, XS), slot_of(0, k, False, PS))
                    if needed(index - PS + 1):
                        dve.wait_ge(groups_done, index - PS + 1)
                    dve.wait_ge(shift_loaded[xs], 16 * SPT * ((m + 1) if start else m))
                    nc.vector.tensor_tensor(
                        products[0:PK, pslot, 0:tiles, :], factors[0:PK, xs, 0:tiles, :],
                        rows3[:, None, :].to_broadcast([PK, tiles, CW]), ALU.mult).then_inc(products_ready, 1)

            def multiply_l1(n, last, k):
                index = l1_index(n, k, last)
                xs, pslot = slot_of(1, k, last, XS), slot_of(1, k, last, PS)
                tiles = L1_TILES[k]
                dve.wait_ge(xb_loaded[xs], 16 * l1_loads_before(n, k, last))
                dve.wait_ge(groups_done, index - PS + 1)
                nc.vector.tensor_tensor(
                    products[:, pslot, 0:tiles, :], factors[:, xs, 0:tiles, :],
                    x1[:, None, :].to_broadcast([128, tiles, CW]), ALU.mult).then_inc(products_ready, 1)

            def low_half(n, last, k):
                pslot = slot_of(1, k, last, PS)
                dve.wait_ge(hi_ready, L1G * n + k + 1)
                nc.vector.tensor_tensor(
                    halves_lo[:, k % HS, :, :], products[:, pslot, 0:SPLIT, :],
                    halves_hi[:, k % HS, :, :].bitcast(F32), ALU.subtract).then_inc(lo_ready, 1)

            def low_halves_g(c):
                dve.wait_ge(x2t_hi_ready, c + 1)
                nc.vector.tensor_tensor(x2t_lo[:, :], x2t_ps[:, :], x2t_hi[:, :].bitcast(F32), ALU.subtract
                                        ).then_inc(x2t_lo_ready, 1)
                dve.wait_ge(xt_hi_ready, c + 1)
                nc.vector.tensor_tensor(xt_lo[:, :], xt_ps[:, 0:BLKS * FIELDS], xt_hi[:, :].bitcast(F32),
                                        ALU.subtract).then_inc(xt_lo_ready, 1)

            def sum_d(z_row, c, src, signal):
                nc.vector.tensor_reduce(z[:, z_row, bass.ds(c * CB, CB)], src.rearrange("p (b d) -> p b d", d=D),
                                        AX_X, ALU.add).then_inc(signal, 1)

            def sum_x2(c):
                dve.wait_ge(x2_stored, c + 1)
                sum_d(1, c, x2[:, :], z2_summed)

            def body(n, first=False, last=False):
                if not last:
                    multiply_l0(n + 1)
                if not first:
                    sum_x2(n - 1)
                dve.wait_ge(x1_stored, n + 1)
                for k in range(L1G):
                    multiply_l1(n, last, k)
                    if k >= 1:
                        low_half(n, last, k - 1)
                    if k == 2:
                        if not first:
                            low_halves_g(n - 1)
                        sum_d(0, n, x1[:, :], z1_summed)
                low_half(n, last, L1G - 1)

            multiply_l0(0)
            body(0, first=True)
            with dve.Fori(1, HALF_CHUNKS) as n:
                body(n)
            body(HALF_CHUNKS)
            with dve.Fori(HALF_CHUNKS + 1, CHUNKS - 1) as n:
                body(n)
            body(CHUNKS - 1, last=True)
            sum_x2(CHUNKS - 1)
            low_halves_g(CHUNKS - 1)

        @block.tensor
        def _(pe):
            def layer0(m):
                start = isinstance(m, int) and m == 0
                if start:
                    pe.wait_ge(w0_ready, 1)
                else:
                    pe.wait_ge(x1_stored, m)
                for k, tiles in enumerate(L0_TILES):
                    pslot = k if start else slot_of(0, k, False, PS)
                    pe.wait_ge(products_ready, l0_index(m, k) + 1)
                    for t in range(tiles):
                        tile = first_tile(k) + t
                        parts = PK if tile < QT - 1 else QT_LAST
                        mm = nc.tensor.matmul(quad_ps[:, :], w0_sb[0:parts, tile, :],
                                              products[0:parts, pslot, t, :],
                                              start=(tile == 0), stop=(tile == QT - 1))
                        if t == tiles - 1 and k == 0:
                            mm.then_inc(groups_done, 1)
                mm.then_inc(groups_done, 1)

            def layer1(n, last, k):
                pslot = slot_of(1, k, last, PS)
                pe.wait_ge(products_ready, l1_index(n, k, last) + 1)
                for t in range(SPLIT, L1_TILES[k]):
                    j = first_tile(k) + t
                    nc.tensor.matmul(cubic_ps[:, :], w1_sb[:, NATIVE_J.index(j), :], products[:, pslot, t, :],
                                     start=(k == 0 and t == SPLIT), stop=False)
                pe.wait_ge(hi_ready, L1G * n + k + 1)
                for t in range(SPLIT):
                    js = SPLIT_J.index(first_tile(k) + t)
                    for w in (w1_hi, w1_lo):
                        nc.tensor.matmul(cubic_ps[:, :], w[:, js, :], halves_hi[:, k % HS, t, :],
                                         start=False, stop=False)
                pe.wait_ge(lo_ready, L1G * n + k + 1)
                for t in range(SPLIT):
                    js = SPLIT_J.index(first_tile(k) + t)
                    mm = nc.tensor.matmul(cubic_ps[:, :], w1_hi[:, js, :], halves_lo[:, k % HS, t, :],
                                          start=False, stop=(k == L1G - 1 and t == SPLIT - 1))
                mm.then_inc(groups_done, 1)

            def transposes(c):
                pe.wait_ge(xrow_loaded, 16 * (c + 1))
                pe.wait_ge(x2_stored, c + 1)
                for i in range(BLKS):
                    mm = nc.tensor.transpose(x2t_ps[:, 128 * i:128 * (i + 1)],
                                             x2[:, 128 * i:128 * (i + 1)], ident[:, :])
                mm.then_inc(x2t_ready, 1)
                for i in range(BLKS):
                    mm = nc.tensor.transpose(xt_ps[:, FIELDS * i:FIELDS * (i + 1)],
                                             xrow[:, 128 * i:128 * (i + 1)], ident[0:FIELDS, 0:FIELDS])
                mm.then_inc(xt_ready, 1)

            def g_block(c, i):
                if i == 0:
                    pe.wait_ge(diag_built, c + 1)
                    pe.wait_ge(x2t_lo_ready, c + 1)
                if i >= 2:
                    pe.wait_ge(g_stored, BLKS * c + i - 1)
                for step, (w, x) in enumerate(((x2t_hi, diag_hi), (x2t_lo, diag_hi), (x2t_hi, diag_lo))):
                    mm = nc.tensor.matmul(g_ps[i % 2][:, 0:FIELDS * BLK_B], w[:, 128 * i:128 * (i + 1)],
                                          x[:, i, :, :].rearrange("p j b -> p (j b)"),
                                          start=(step == 0), stop=(step == 2))
                mm.then_inc(g_ready, 1)

            def layer2(half):
                pe.wait_ge(g_stored, BLKS * HALF_CHUNKS * (half + 1))
                for j in range(FIELDS):
                    mm = nc.tensor.matmul(z3_ps[:, 0:HB], w2_sb[:, j, :], g_sb[:, j, :],
                                          start=(j == 0), stop=(j == FIELDS - 1))
                mm.then_inc(z3_ready, 1)

            def body(n, first=False, last=False, then=None):
                if not last:
                    layer0(n + 1)
                if not first:
                    transposes(n - 1)
                else:
                    pe.wait_ge(w1_loaded, 32)
                    pe.wait_ge(w1_lo_ready, 1)
                for k in range(L1G):
                    if k == 0 and not first:
                        pe.wait_ge(x2_stored, n)
                    layer1(n, last, k)
                    if not first and 4 <= k < 4 + BLKS:
                        g_block(n - 1, k - 4)
                    if k == 9 and then is not None:
                        then()

            pe.wait_ge(small_loaded, 48)
            layer0(0)
            body(0, first=True)
            with pe.Fori(1, HALF_CHUNKS) as n:
                body(n)
            pe.wait_ge(late_loaded, 16 * 4)
            body(HALF_CHUNKS, then=lambda: layer2(0))
            with pe.Fori(HALF_CHUNKS + 1, CHUNKS - 1) as n:
                body(n)
            body(CHUNKS - 1, last=True)
            transposes(CHUNKS - 1)
            for i in range(BLKS):
                g_block(CHUNKS - 1, i)
            layer2(1)

            banks = [quad_ps, cubic_ps, xt_ps, x2t_ps]
            pe.wait_ge(mlp_loaded, 64)
            pe.wait_ge(z1_summed, CHUNKS)
            pe.wait_ge(z2_summed, CHUNKS)
            for mt in range(N1 // 128):
                cols = slice(128 * mt, 128 * (mt + 1))
                nc.tensor.matmul(banks[mt][:, :], wt1_sb[:, 0, cols], z[:, 0, :], start=True, stop=False)
                nc.tensor.matmul(banks[mt][:, :], wt1_sb[:, 1, cols], z[:, 1, :], start=False, stop=False)
                nc.tensor.matmul(banks[mt][:, :], wt1c_sb[:, cols], ctx_sb[:, :], start=False, stop=False)
            pe.wait_ge(z3_stored, 2)
            for mt in range(N1 // 128):
                nc.tensor.matmul(banks[mt][:, :], wt1_sb[:, 2, 128 * mt:128 * (mt + 1)], z[:, 2, :],
                                 start=False, stop=True).then_inc(mlp_ready, 1)
            for mt in range(N2 // 128):
                for kt in range(N1 // 128):
                    if mt == 0:
                        pe.wait_ge(mlp_stored, kt + 1)
                    mm = nc.tensor.matmul(g_ps[mt][:, :], wt2_sb[:, kt, 128 * mt:128 * (mt + 1)], h1[:, kt, :],
                                          start=(kt == 0), stop=(kt == N1 // 128 - 1))
                mm.then_inc(mlp_ready, 1)
            for kt in range(N2 // 128):
                pe.wait_ge(mlp_stored, N1 // 128 + kt + 1)
                mm = nc.tensor.matmul(y_ps[0:1, :], wt3_sb[:, kt:kt + 1], h2[:, kt, :],
                                      start=(kt == 0), stop=(kt == N2 // 128 - 1))
            mm.then_inc(mlp_ready, 1)

        @block.scalar
        def _(act):
            def store_x1(m):
                if not (isinstance(m, int) and m == 0):
                    act.wait_ge(products_ready, l1_index(m - 1, L1G - 1, False) + 1)
                    act.wait_ge(z1_summed, m)
                act.wait_ge(groups_done, l0_index(m, L0G - 1) + 1)
                nc.scalar.activation(x1[:, :], quad_ps[:, :], ACT.Identity, bias=bias_sb[:, 0:1]
                                     ).then_inc(x1_stored, 1)

            def store_x2(c, last=False):
                act.wait_ge(groups_done, l1_index(c, L1G - 1, last) + 1)
                nc.scalar.activation(x2[:, :], cubic_ps[:, :], ACT.Identity, bias=bias_sb[:, 1:2]
                                     ).then_inc(x2_stored, 1)

            def high_halves_g(c):
                act.wait_ge(x2t_ready, c + 1)
                nc.scalar.copy(x2t_hi[:, :], x2t_ps[:, :]).then_inc(x2t_hi_ready, 1)
                act.wait_ge(xt_ready, c + 1)
                nc.scalar.copy(xt_hi[:, :], xt_ps[:, 0:BLKS * FIELDS]).then_inc(xt_hi_ready, 1)

            def build_diag(dst, src):
                src = src.rearrange("p (i j) -> p i j", j=FIELDS)
                for b in range(BLK_B):
                    last = nc.scalar.activation(dst[:, :, :, b], src, ACT.Copy, scale=mask[:, b:b + 1])
                return last

            def high_half(n, last, k):
                act.wait_ge(products_ready, l1_index(n, k, last) + 1)
                if not (isinstance(n, int) and n == 0 and k < HS):
                    before = l1_index(n, k - HS, last) if k >= HS else l1_index(n - 1, k - HS + L1G, False)
                    act.wait_ge(groups_done, before + 1)
                nc.scalar.copy(halves_hi[:, k % HS, :, :], products[:, slot_of(1, k, last, PS), 0:SPLIT, :]
                               ).then_inc(hi_ready, 1)

            def store_g(c, half, i):
                act.wait_ge(g_ready, BLKS * c + i + 1)
                nc.scalar.copy(g_sb[:, :, bass.ds(c * CB + (i * BLK_B - half * HB), BLK_B)],
                               g_ps[i % 2][:, 0:FIELDS * BLK_B].rearrange("p (j b) -> p j b", b=BLK_B)
                               ).then_inc(g_stored, 1)

            def store_z3(half):
                act.wait_ge(z3_ready, half + 1)
                nc.scalar.activation(z[:, 2, HB * half:HB * (half + 1)], z3_ps[:, 0:HB], ACT.Identity,
                                     bias=bias2d[:, :]).then_inc(z3_stored, 1)

            def body(n, half, first=False, last=False):
                if not first:
                    store_x2(n - 1)
                for k in range(L1G):
                    high_half(n, last, k)
                    if not first:
                        if k == 1:
                            high_halves_g(n - 1)
                        if k == 2:
                            act.wait_ge(xt_hi_ready, n)
                            build_diag(diag_hi, xt_hi[:, :].bitcast(F32))
                        if k == 3:
                            act.wait_ge(xt_lo_ready, n)
                            build_diag(diag_lo, xt_lo[:, :]).then_inc(diag_built, 1)
                        if 6 <= k < 6 + BLKS:
                            store_g(n - 1, half, k - 6)
                if not last:
                    store_x1(n + 1)

            act.wait_ge(small_loaded, 48)
            act.wait_ge(w1_loaded, 32)
            nc.scalar.copy(w1_hi[:, :, :], w1s_sb).then_inc(w1_hi_ready, 1)
            act.wait_ge(bias_ready, 1)
            store_x1(0)
            body(0, 0, first=True)
            act.wait_ge(w1_lo_ready, 1)
            with act.Fori(1, HALF_CHUNKS) as n:
                body(n, 0)
            body(HALF_CHUNKS, 0)
            store_z3(0)
            with act.Fori(HALF_CHUNKS + 1, CHUNKS - 1) as n:
                body(n, 1)
            body(CHUNKS - 1, 1, last=True)
            store_x2(CHUNKS - 1, last=True)
            high_halves_g(CHUNKS - 1)
            act.wait_ge(xt_hi_ready, CHUNKS)
            build_diag(diag_hi, xt_hi[:, :].bitcast(F32))
            act.wait_ge(xt_lo_ready, CHUNKS)
            build_diag(diag_lo, xt_lo[:, :]).then_inc(diag_built, 1)
            for i in range(BLKS):
                store_g(CHUNKS - 1, 1, i)
            store_z3(1)
            banks = [quad_ps, cubic_ps, xt_ps, x2t_ps]
            for mt in range(N1 // 128):
                act.wait_ge(mlp_ready, mt + 1)
                nc.scalar.activation(h1[:, mt, :], banks[mt][:, :], ACT.Relu, bias=bt1_sb[:, mt:mt + 1]
                                     ).then_inc(mlp_stored, 1)
            for mt in range(N2 // 128):
                act.wait_ge(mlp_ready, N1 // 128 + mt + 1)
                nc.scalar.activation(h2[:, mt, :], g_ps[mt][:, :], ACT.Relu, bias=bt2_sb[:, mt:mt + 1]
                                     ).then_inc(mlp_stored, 1)
            act.wait_ge(mlp_ready, N1 // 128 + N2 // 128 + 1)
            nc.scalar.copy(y_sb[:, :], y_ps[0:1, :]).then_inc(mlp_stored, 1)


def kernel(**inputs):
    import concourse.bacc as bacc
    from concourse.bass_utils import run_bass_kernel_spmd

    a = {k: np.asarray(v) for k, v in inputs.items()}
    ids = np.zeros((GATHERS * FPG, B), np.int32)
    ids[:FIELDS] = a["ids"].T
    ids = ids.reshape(GATHERS, FPG, CHUNKS, CB).transpose(1, 3, 2, 0).reshape(128, CHUNKS, GATHERS)
    first = np.zeros(GATHERS * FPG, np.int32)
    first[:FIELDS] = np.concatenate([[0], np.cumsum(VOCABS)[:-1]])
    bases = np.repeat(first.reshape(GATHERS, FPG).T, CB, axis=0)
    tables = np.concatenate([a[f"tbl_{f}"] for f in range(FIELDS)], axis=0)
    w0 = a["L0_rec_W0"].reshape(H, FIELDS, FIELDS)
    j = np.arange(FIELDS)[None, :, None]
    s = np.arange(SPT)[:, None, None] + SPT * np.arange(QT)[None, None, :]
    k = (j + s) % FIELDS
    j = np.broadcast_to(j, k.shape)
    w0a = w0[:, j, k].transpose(1, 2, 3, 0).reshape(PK, QT, H)
    w0b = w0[:, k, j].transpose(1, 2, 3, 0).reshape(PK, QT, H).copy()
    w0b[:FIELDS, 0] = 0
    by_j = lambda w: w.reshape(H, FIELDS, H).transpose(2, 1, 0)
    mask = (np.arange(128)[:, None] // D == np.arange(BLK_B)[None, :]).astype(np.float32)
    arrays = {
        "ids": ids, "bases": bases, "tables": tables, "w0a": w0a, "w0b": w0b,
        "w1n": by_j(a["L0_rec_W1"])[:, NATIVE_J], "w1s": by_j(a["L0_rec_W1"])[:, SPLIT_J], "w2": by_j(a["L0_rec_W2"]),
        "biases": np.stack([a[f"L0_rec_b{i}"] for i in range(3)], axis=1),
        "ctx_in": a["dense_ctx"].T,
        "wt1": a["W_top1"][:3 * 128].reshape(3, 128, N1).transpose(1, 0, 2), "wt1c": a["W_top1"][3 * 128:],
        "bt1": a["b_top1"].reshape(N1 // 128, 128).T,
        "wt2": a["W_top2"].reshape(N1 // 128, 128, N2).transpose(1, 0, 2),
        "bt2": a["b_top2"].reshape(N2 // 128, 128).T, "wt3": a["W_top3"].reshape(N2 // 128, 128).T,
        "ident_in": np.eye(128, dtype=np.float32), "mask_in": mask,
    }
    arrays = {f"{k}_dram": np.ascontiguousarray(v) for k, v in arrays.items()}
    nc = bacc.Bacc("TRN2", target_bir_lowering=False, num_devices=1)
    aps = {n.removesuffix("_dram"): nc.dram_tensor(n, v.shape, mybir.dt.from_np(v.dtype), kind="ExternalInput").ap()
           for n, v in arrays.items()}
    aps["x_rows"] = nc.dram_tensor("x_rows", (X_ROWS, COLS), F32, kind="Internal").ap()
    aps["out"] = nc.dram_tensor("out_dram", (1, B), F32, kind="ExternalOutput").ap()
    build(nc, **aps)
    r = run_bass_kernel_spmd(nc, [arrays], core_ids=[0])
    return r.results[0]["out_dram"].reshape(B, 1)
```

```python
from contextlib import ExitStack

import numpy as np

import concourse.bass as bass
from concourse import mybir

F32 = mybir.dt.float32
F32R = mybir.dt.float32r
I32 = mybir.dt.int32
ALU = mybir.AluOpType
ACT = mybir.ActivationFunctionType
AX_X = mybir.AxisListType.X

VOCABS = [12500, 12500, 1000, 1250, 1250, 1000, 1250, 125000, 125000, 1000, 125000, 125000, 1250,
          125000, 1250, 1000, 1250, 12500, 1000, 12500, 125000, 1250, 1250, 12500, 1000, 1000, 12500,
          1250, 12500, 125000, 125000, 12500, 125000, 125000, 1250, 12500, 12500, 1250, 1000]
B, FIELDS, D, H = 512, 39, 16, 128
CTX = 16
N1, N2 = 512, 256
COLS = B * D
CW = 512
CHUNKS = COLS // CW
CB = CW // D
HALF_CHUNKS = CHUNKS // 2
HB = B // 2
BLK_B = 128 // D
BLKS = CW // 128
PAIRS = BLKS // 2
PW = 2 * 128
SHIFTS = FIELDS // 2 + 1
SPT = 128 // FIELDS
PK = SPT * FIELDS
QT = -(-SHIFTS // SPT)
QT_LAST = (SHIFTS - (QT - 1) * SPT) * FIELDS
X_ROWS = SPT * QT - 1 + FIELDS
DUP = X_ROWS - FIELDS
GF = 512 // H
GROUPS = -(-FIELDS // GF)
RING = 2
STAGES = 4
ADDS = GROUPS - 2
PARTS = [(0, HALF_CHUNKS), (HALF_CHUNKS, CHUNKS - 4), (CHUNKS - 4, CHUNKS)]
FPG = 128 // CB
GATHERS = -(-FIELDS // FPG)
HALF_G = GATHERS // 2
DUP_G = DUP // FPG
GATHER_AT = ({0: 0, 2: 1, 4: 2, 6: 3, 8: 4}, {0: 5, 1: 6, 3: 7, 5: 8, 7: 9})
L0_PRODUCT_AT = ({1: 0, 3: 4, 5: 5, 7: 1, 9: 6}, {1: 2, 3: 3})
L0_VECTOR_AT = ({}, {0: 5, 1: 1, 3: 6, 5: 2, 7: 3})
L0_POOL_AT = ({8: 0}, {6: 4})
L0_HIGH_AT, L0_LOW_AT = {1: 1, 5: 2, 7: 3}, {3: 1, 7: 2, 9: 3}
TENSOR_TILES = [t for at in L0_PRODUCT_AT for t in at.values()]
VECTOR_TILES = [t for at in L0_VECTOR_AT for t in at.values()]
POOL_TILES = [t for at in L0_POOL_AT for t in at.values()]
START_TILES = [0, 1, 4, 2, 5, 3, 6]
SPLIT_TILES = sorted(L0_HIGH_AT.values())
STARTS = 2
COMBINE_AT = 1
W2_STEP = FIELDS // HALF_CHUNKS + 1
W2_FIRST = FIELDS - W2_STEP * (HALF_CHUNKS - 1)
G_AT = {6: 0, 9: 1}
TRANSPOSE_AT = 6


def fields_of(g):
    return range(g * GF, min(FIELDS, (g + 1) * GF))


def is_zero(count):
    return isinstance(count, int) and count == 0


assert GROUPS % RING == 0 and (GROUPS - 2) % STAGES == 0 and len(fields_of(GROUPS - 1)) == GF - 1
assert DUP_G == HALF_G and W2_FIRST > 0


def build(nc, ids, bases, tables, x_rows, w0a, w0b, w1, w2, biases, b1_row, ctx_in, wt1, wt1c, bt1, wt2, bt2, wt3,
          ident_in, mask_in, out):
    with ExitStack() as stack:
        def sb(name, shape, dt=F32):
            return stack.enter_context(nc.sbuf_tensor(name, shape, dt))

        def ps(name):
            return stack.enter_context(nc.psum_tensor(name, [128, 512], F32))

        def sem(name):
            return stack.enter_context(nc.semaphore(name))

        ids_sb = sb("ids_sb", [128, CHUNKS, GATHERS], I32)
        bases_sb = sb("bases_sb", [128, GATHERS], I32)
        rows_now = sb("rows_now", [128, 3, GATHERS], I32)
        passed = sb("passed", [128, 1], I32)
        emb = sb("emb", [128, 3, GATHERS, D])
        w0_sb = sb("w0_sb", [PK, QT, H])
        w1_hi = sb("w1_hi", [128, FIELDS, H], F32R)
        w1_lo = sb("w1_lo", [128, FIELDS, H], F32R)
        w2_sb = sb("w2_sb", [128, FIELDS, H])
        bias_sb = sb("bias_sb", [128, 3])
        bias2d = sb("bias2d", [128, 1])
        no_bias = sb("no_bias", [128, H])
        bt1_sb = sb("bt1_sb", [128, N1 // 128])
        bt2_sb = sb("bt2_sb", [128, N2 // 128])
        wt3_sb = sb("wt3_sb", [128, N2 // 128])
        ident = sb("ident", [128, 128])
        mask = sb("mask", [128, BLK_B])
        shifted = sb("shifted", [128, QT, CW])
        products_hi = sb("products_hi", [PK, len(SPLIT_TILES), CW], F32R)
        products_lo = sb("products_lo", [PK, len(SPLIT_TILES), CW], F32R)
        w0_lo = sb("w0_lo", [PK, len(SPLIT_TILES), H], F32R)
        w0_hi = sb("w0_hi", [PK, len(SPLIT_TILES), H], F32R)
        rows3 = sb("rows3", [PK, CW])
        products = sb("products", [128, QT, CW])
        x1 = sb("x1", [128, CW])
        x1_hi = sb("x1_hi", [128, CW], F32R)
        x1_lo = sb("x1_lo", [128, CW], F32R)
        xrow = sb("xrow", [FIELDS, CW])
        xt = sb("xt", [128, BLKS, FIELDS])
        staged = sb("staged", [128, STAGES, GF, H])
        staged_last = sb("staged_last", [128, GF, H])
        sums = sb("sums", [128, PAIRS, GF, H])
        acc = sb("acc", [128, PAIRS, 2, 2, H])
        x2t = sb("x2t", [128, 2, H])
        x2t_hi = sb("x2t_hi", [128, 2, H], F32R)
        x2t_lo = sb("x2t_lo", [128, 2, H], F32R)
        diag = sb("diag", [128, BLKS, BLK_B, FIELDS + 1])
        diag_hi = sb("diag_hi", [128, BLKS, BLK_B, FIELDS + 1], F32R)
        diag_lo = sb("diag_lo", [128, BLKS, BLK_B, FIELDS + 1], F32R)
        g_sb = sb("g_sb", [128, FIELDS, HB])
        z = sb("z", [128, 3, B])
        w1_sb = g_sb[:, :, 0:H]
        w0b_sb = g_sb[0:PK, 0:QT, H:2 * H]
        h1 = products[:, 0:N1 // 128, :]
        h2 = products[:, N1 // 128:N1 // 128 + N2 // 128, :]
        y_sb = products[0:1, N1 // 128 + N2 // 128, :]
        wt1_sb = shifted[:, 0:3, :]
        wt2_sb = shifted[:, 3:5, :].rearrange("p a (t n) -> p (a t) n", n=N2)
        wt1c_sb, ctx_sb = shifted[0:CTX, 5, :], shifted[0:CTX, 6, :]
        b1_rows = staged_last[:, GF - 1, :]

        quad_ps, xt_ps, g_ps, z3_ps = ps("quad_ps"), ps("xt_ps"), ps("g_ps"), ps("z3_ps")
        a_ps = [[ps(f"a_ps{s}{r}") for r in range(RING)] for s in range(2)]

        ids_loaded = sem("ids_loaded")
        rows_picked = sem("rows_picked")
        gathered = [sem("gathered_first"), sem("gathered_second")]
        written = [sem("written_first"), sem("written_second")]
        w0_loaded, w1_loaded, late_loaded, small_loaded = (
            sem("w0_loaded"), sem("w1_loaded"), sem("late_loaded"), sem("small_loaded"))
        w0_ready, bias_ready = sem("w0_ready"), sem("bias_ready")
        w1_hi_ready, w1_lo_ready = sem("w1_hi_ready"), sem("w1_lo_ready")
        diag_zeroed, diag_set = sem("diag_zeroed"), sem("diag_set")
        x_loaded, xrow_loaded = sem("x_loaded"), sem("xrow_loaded")
        vector_products, pool_products = sem("vector_products"), sem("pool_products")
        products_hi_ready, products_lo_ready = sem("products_hi_ready"), sem("products_lo_ready")
        w0_folded, w0_hi_ready = sem("w0_folded"), sem("w0_hi_ready")
        products_used = sem("products_used")
        x1_stored, x1_hi_ready, x1_lo_ready = sem("x1_stored"), sem("x1_hi_ready"), sem("x1_lo_ready")
        transposed, xt_ready = sem("transposed"), sem("xt_ready")
        diag_copied = [sem("diag_copied_first"), sem("diag_copied_second")]
        diag_hi_ready, diag_lo_ready = sem("diag_hi_ready"), sem("diag_lo_ready")
        filled = [sem("filled_first"), sem("filled_second")]
        vector_added, pool_added = sem("vector_added"), sem("pool_added")
        staged_ready = sem("staged_ready")
        last_added, folded = sem("last_added"), sem("folded")
        x2t_ready, x2t_hi_ready, x2t_lo_ready = sem("x2t_ready"), sem("x2t_hi_ready"), sem("x2t_lo_ready")
        g_ready, g_stored = sem("g_ready"), sem("g_stored")
        z1_summed = sem("z1_summed")
        z3_ready, z3_stored = sem("z3_ready"), sem("z3_stored")
        mlp_ready, mlp_stored = sem("mlp_ready"), sem("mlp_stored")
        mlp_loaded = sem("mlp_loaded")
        out_written = sem("out_written")

        block = stack.enter_context(nc.Block())

        def wait_product(engine, m, t):
            if isinstance(m, int) and m < STARTS:
                engine.wait_ge(vector_products, QT * m + START_TILES.index(t) + 1)
            elif t in POOL_TILES:
                engine.wait_ge(pool_products, len(POOL_TILES) * (m - STARTS) + POOL_TILES.index(t) + 1)
            else:
                before = STARTS * (QT - len(VECTOR_TILES))
                engine.wait_ge(vector_products, len(VECTOR_TILES) * m + before + VECTOR_TILES.index(t) + 1)

        def multiply_l0(engine, m, t, signal):
            engine.wait_ge(x_loaded, 16 * 2 * SPT * (m + 1))
            if not is_zero(m):
                engine.wait_ge(products_used, QT * (m - 1) + TENSOR_TILES.index(t) + 1)
            engine.tensor_tensor(products[0:PK, t, :], shifted[0:PK, t, :], rows3[:, :], ALU.mult
                                 ).then_inc(signal, 1)

        @block.gpsimd
        def _(pool):
            pool.wait_ge(ids_loaded, 32)

            def pick_rows(m, buf):
                ids_now = ids_sb[:, bass.ds(m, 1), :].rearrange("p a g -> p (a g)")
                nc.gpsimd.tensor_tensor(rows_now[:, buf, :], ids_now, bases_sb[:, :], ALU.add
                                        ).then_inc(rows_picked, 1)
                pool.wait_ge(rows_picked, m + 1)
                nc.gpsimd.tensor_tensor(passed[:, :], bases_sb[:, 0:1], bases_sb[:, 0:1], ALU.add)

            def gather(buf, g):
                parts = CB * min(FPG, FIELDS - g * FPG)
                nc.gpsimd.indirect_dma_start(
                    out=emb[0:parts, buf, g, :], out_offset=None, in_=tables[:, :],
                    in_offset=bass.IndirectOffsetOnAxis(ap=rows_now[0:parts, buf, g:g + 1], axis=0),
                ).then_inc(gathered[g // HALF_G], 16)

            def body(n, gathering=True, multiplying=True):
                for pair in range(PAIRS):
                    q = PAIRS * n + pair
                    for g in range(GROUPS):
                        if 0 < g <= ADDS:
                            pool.wait_ge(staged_ready, GROUPS * q + g + 1)
                            if g > 1:
                                pool.wait_ge(pool_added, ADDS * q + g - 1)
                            nc.gpsimd.tensor_tensor(sums[:, pair, :, :], sums[:, pair, :, :],
                                                    staged[:, (g - 1) % STAGES, :, :], ALU.add
                                                    ).then_inc(pool_added, 1)
                        if multiplying and g in L0_POOL_AT[pair]:
                            multiply_l0(nc.gpsimd, n + 2, L0_POOL_AT[pair][g], pool_products)
                        step = GATHER_AT[pair].get(g)
                        if gathering and step is not None:
                            if step in (0, HALF_G):
                                half = step // HALF_G
                                pool.wait_ge(gathered[half], 16 * HALF_G * (n + 3))
                                pool.wait_ge(written[half], 16 * (2 - half) * FPG * (n + 3))
                                if half == 0:
                                    pool.wait_ge(gathered[1], 16 * HALF_G * (n + 3))
                                    pick_rows(n + 3, 2)
                                else:
                                    nc.gpsimd.tensor_tensor(passed[:, :], bases_sb[:, 0:1], bases_sb[:, 0:1],
                                                            ALU.add)
                            gather(2, step)

            for m in range(3):
                if m > 0:
                    pool.wait_ge(gathered[0], 16 * HALF_G * m)
                    pool.wait_ge(gathered[1], 16 * HALF_G * m)
                pick_rows(m, m)
                for g in range(GATHERS):
                    gather(m, g)
            pool.wait_ge(small_loaded, 64)
            body(0)
            with pool.Fori(1, CHUNKS - 3) as n:
                body(n)
            body(CHUNKS - 3, gathering=False)
            with pool.Fori(CHUNKS - 2, CHUNKS) as n:
                body(n, gathering=False, multiplying=False)

        @block.sync
        def _(sp):
            def value(count):
                return count if isinstance(count, int) else sp.snap(sp.to_reg(count))

            def write_x(m, half, buf):
                sp.wait_ge(gathered[half], 16 * HALF_G * (m + 1))
                for f in range(FPG):
                    full = GATHERS - 1 + (f < FIELDS - FPG * (GATHERS - 1))
                    lo, hi = (0, HALF_G) if half == 0 else (HALF_G, full)
                    src = emb[CB * f:CB * (f + 1), buf, lo:hi, :]
                    for row in ((f, FIELDS + f) if half == 0 else (f + FPG * HALF_G,)):
                        dst = x_rows[row:row + FPG * (hi - lo - 1) + 1:FPG, bass.ds(m * CW, CW)]
                        sp.dma_start(dst.rearrange("g (b d) -> b g d", d=D), src).then_inc(written[half], 16)

            def load_x(m):
                first_half, second_half = value(16 * 2 * FPG * (m + 1)), value(16 * FPG * (m + 1))
                start = isinstance(m, int) and m <= STARTS
                of_vector = value(QT * m if start else len(VECTOR_TILES) * m + STARTS * (QT - len(VECTOR_TILES)))
                of_pool = value(0 if start else len(POOL_TILES) * (m - STARTS))
                sp.wait_ge(written[0], first_half)
                sp.wait_ge(written[1], second_half)
                if not is_zero(m):
                    sp.wait_ge(vector_products, of_vector)
                if not start:
                    sp.wait_ge(pool_products, of_pool)
                for s in reversed(range(SPT)):
                    src = bass.AP(x_rows.tensor, s * COLS + m * CW, [[COLS, FIELDS], [SPT * COLS, QT], [1, CW]])
                    sp.dma_start(shifted[FIELDS * s:FIELDS * (s + 1), :, :], src).then_inc(x_loaded, 16)
                    sp.dma_start(rows3[FIELDS * s:FIELDS * (s + 1), :], x_rows[0:FIELDS, bass.ds(m * CW, CW)]
                                 ).then_inc(x_loaded, 16)

            def load_xrow(m):
                if not is_zero(m):
                    sp.wait_ge(transposed, m)
                sp.dma_start(xrow[:, :], x_rows[0:FIELDS, bass.ds(m * CW, CW)]).then_inc(xrow_loaded, 16)

            def copy_diag(q, pair):
                transposed_now, taken_before = value(q + 1), value(q - 1)
                sp.wait_ge(xt_ready, transposed_now)
                if not (isinstance(q, int) and q < 2):
                    sp.wait_ge(diag_lo_ready, taken_before)
                blks = slice(2 * pair, 2 * pair + 2)
                for b in range(BLK_B):
                    rows = slice(D * b, D * (b + 1))
                    sp.dma_start(diag[rows, blks, b, 0:FIELDS], xt[rows, blks, :]).then_inc(diag_copied[pair], 16)

            sp.dma_start(ids_sb[:, :, :], ids).then_inc(ids_loaded, 16)
            sp.dma_start(bases_sb[:, :], bases).then_inc(ids_loaded, 16)
            sp.dma_start(w0_sb[:, :, :], w0a).then_inc(w0_loaded, 16)
            sp.dma_start(w0b_sb, w0b).then_inc(w0_loaded, 16)
            sp.dma_start(bias_sb[:, :], biases).then_inc(small_loaded, 16)
            sp.dma_start(ident[:, :], ident_in).then_inc(small_loaded, 16)
            sp.dma_start(mask[:, :], mask_in).then_inc(small_loaded, 16)
            sp.dma_start(b1_rows, b1_row.to_broadcast([128, H])).then_inc(small_loaded, 16)
            sp.dma_start(w1_sb, w1).then_inc(w1_loaded, 16)
            for m in range(2):
                write_x(m, 0, m)
                write_x(m, 1, m)
                load_x(m)
                if m == 0:
                    load_xrow(0)
            write_x(2, 0, 2)
            sp.wait_ge(diag_set, 1)
            copy_diag(0, 0)

            def body(n, loading=True, writing=True, last=False):
                if loading:
                    write_x(n + 2, 1, 2)
                    load_x(n + 2)
                copy_diag(PAIRS * n + 1, 1)
                if last:
                    return
                load_xrow(n + 1)
                if writing:
                    write_x(n + 3, 0, 2)
                copy_diag(PAIRS * (n + 1), 0)

            body(0)
            late = ((bt1_sb[:, :], bt1), (bt2_sb[:, :], bt2), (wt3_sb[:, :], wt3))
            for dst, src in late:
                sp.dma_start(dst, src).then_inc(late_loaded, 16)

            def load_w2(j, count):
                sp.dma_start(w2_sb[:, bass.ds(j, count), :], w2[:, bass.ds(j, count), :]).then_inc(late_loaded, 16)

            load_w2(0, W2_FIRST)
            with sp.Fori(1, HALF_CHUNKS) as n:
                body(n)
                load_w2(n * W2_STEP - (W2_STEP - W2_FIRST), W2_STEP)
            with sp.Fori(HALF_CHUNKS, CHUNKS - 3) as n:
                body(n)
            body(CHUNKS - 3, writing=False)
            body(CHUNKS - 2, loading=False, writing=False)
            body(CHUNKS - 1, loading=False, writing=False, last=True)
            for t in (VECTOR_TILES[-1], POOL_TILES[-1]):
                wait_product(sp, CHUNKS - 1, t)
            for dst, src in ((wt1_sb, wt1), (wt1c_sb, wt1c), (wt2_sb, wt2), (ctx_sb, ctx_in)):
                sp.dma_start(dst, src).then_inc(mlp_loaded, 16)
            sp.wait_ge(mlp_stored, N1 // 128 + N2 // 128 + 1)
            sp.dma_start(out, y_sb[:, :]).then_inc(out_written, 16)
            sp.wait_ge(out_written, 16)

        @block.vector
        def _(dve):
            dve.wait_ge(w0_loaded, 32)
            nc.vector.tensor_tensor(w0_sb[:, :, :], w0_sb[:, :, :], w0b_sb, ALU.add
                                    ).then_inc(w0_folded, 1)
            nc.vector.memset(no_bias[:, :], 0.0)
            nc.vector.memset(diag[:, :, :, :], 0.0).then_inc(diag_zeroed, 1)
            dve.wait_ge(small_loaded, 64)
            nc.vector.tensor_scalar(bias2d[:, :], bias_sb[:, 2:3], float(D), None, ALU.mult
                                    ).then_inc(bias_ready, 1)
            dve.wait_ge(w0_hi_ready, 1)
            for i, t in enumerate(SPLIT_TILES):
                last = nc.vector.tensor_tensor(w0_lo[:, i, :], w0_sb[:, t, :], w0_hi[:, i, :].bitcast(F32), ALU.subtract)
            last.then_inc(w0_ready, 1)

            def low_product(m, t):
                i = SPLIT_TILES.index(t)
                dve.wait_ge(products_hi_ready, len(SPLIT_TILES) * m + i + 1)
                nc.vector.tensor_tensor(products_lo[:, i, :], products[0:PK, t, :], products_hi[:, i, :].bitcast(F32),
                                        ALU.subtract).then_inc(products_lo_ready, 1)

            def low_x1(n, pair):
                cols = slice(PW * pair, PW * (pair + 1))
                dve.wait_ge(x1_hi_ready, PAIRS * n + pair + 1)
                nc.vector.tensor_tensor(x1_lo[:, cols], x1[:, cols], x1_hi[:, cols].bitcast(F32), ALU.subtract
                                        ).then_inc(x1_lo_ready, 1)

            def low_diag(q, pair):
                blks = slice(2 * pair, 2 * pair + 2)
                dve.wait_ge(diag_hi_ready, q + 1)
                nc.vector.tensor_tensor(diag_lo[:, blks, :, :], diag[:, blks, :, :],
                                        diag_hi[:, blks, :, :].bitcast(F32), ALU.subtract).then_inc(diag_lo_ready, 1)

            def add_group(q, pair, g):
                dve.wait_ge(filled[0], GROUPS * q + g + 1)
                if g == 0:
                    dve.wait_ge(xt_ready, q + 1)
                    if not (isinstance(q, int) and q < 2):
                        dve.wait_ge(x2t_ready, q - 1)
                for j in fields_of(g):
                    if j >= 2:
                        dve.wait_ge(vector_added, FIELDS * q + j - 1)
                    before = b1_rows if j == 0 else no_bias[:, :] if j == 1 else acc[:, pair, j % 2, 0, :]
                    nc.vector.scalar_tensor_tensor(
                        acc[:, pair, j % 2, 0, :], a_ps[0][g % RING][:, H * (j % GF):H * (j % GF + 1)],
                        xt[:, 2 * pair, j:j + 1], before, ALU.mult, ALU.add).then_inc(vector_added, 1)

            def add_last(q, pair):
                dve.wait_ge(staged_ready, GROUPS * (q + 1))
                dve.wait_ge(pool_added, ADDS * (q + 1))
                nc.vector.tensor_tensor(sums[:, pair, :, :], sums[:, pair, :, :], staged_last[:, :, :], ALU.add
                                        ).then_inc(last_added, 1)

            def combine(q, pair):
                dve.wait_ge(last_added, q + 1)
                nc.vector.tensor_tensor(acc[:, pair, :, 1, :], sums[:, pair, 0:2, :], sums[:, pair, 2:4, :], ALU.add
                                        ).then_inc(folded, 1)
                dve.wait_ge(folded, q + 1)
                dve.wait_ge(vector_added, FIELDS * (q + 1))
                if not is_zero(q):
                    dve.wait_ge(x2t_hi_ready, q)
                nc.vector.tensor_tensor(x2t[:, :, :], acc[:, pair, 0, :, :], acc[:, pair, 1, :, :], ALU.add
                                        ).then_inc(x2t_ready, 1)

            def low_x2t(q):
                dve.wait_ge(x2t_hi_ready, q + 1)
                nc.vector.tensor_tensor(x2t_lo[:, :, :], x2t[:, :, :], x2t_hi[:, :, :].bitcast(F32), ALU.subtract
                                        ).then_inc(x2t_lo_ready, 1)

            def sum_x1(n):
                dve.wait_ge(x1_stored, n + 1)
                nc.vector.tensor_reduce(z[:, 0, bass.ds(n * CB, CB)], x1[:, :].rearrange("p (b d) -> p b d", d=D),
                                        AX_X, ALU.add).then_inc(z1_summed, 1)

            def body(n, first=False, last=False, multiplying=True):
                for pair in range(PAIRS):
                    q = PAIRS * n + pair
                    for g in range(GROUPS):
                        add_group(q, pair, g)
                        if first and pair == 0 and g < QT:
                            multiply_l0(nc.vector, 1, START_TILES[g], vector_products)
                        if multiplying and g in L0_VECTOR_AT[pair]:
                            multiply_l0(nc.vector, n + 2, L0_VECTOR_AT[pair][g], vector_products)
                        if not last and pair == 0 and g in L0_LOW_AT:
                            low_product(n + 1, L0_LOW_AT[g])
                        if g == COMBINE_AT and not (first and pair == 0):
                            add_last(q - 1, 1 - pair)
                        if g == COMBINE_AT + 1 and not (first and pair == 0):
                            combine(q - 1, 1 - pair)
                        if g == COMBINE_AT + 3 and not (first and pair == 0):
                            low_x2t(q - 1)
                        if pair == 0:
                            if g == 1:
                                low_x1(n, 1)
                        elif g == 7 and not last:
                            low_x1(n + 1, 0)
                        elif g == 9 and not last:
                            sum_x1(n + 1)
                        if g == 6:
                            low_diag(q, pair)

            for part in range(3):
                j0, j1 = FIELDS * part // 3, FIELDS * (part + 1) // 3
                dve.wait_ge(w1_hi_ready, part + 1)
                nc.vector.tensor_tensor(w1_lo[:, j0:j1, :], w1_sb[:, j0:j1, :], w1_hi[:, j0:j1, :].bitcast(F32),
                                        ALU.subtract).then_inc(w1_lo_ready, 1)
            for t in START_TILES:
                multiply_l0(nc.vector, 0, t, vector_products)
            for t in SPLIT_TILES:
                low_product(0, t)
            low_x1(0, 0)
            sum_x1(0)
            body(0, first=True)
            with dve.Fori(1, CHUNKS - 2) as n:
                body(n)
            body(CHUNKS - 2, multiplying=False)
            body(CHUNKS - 1, last=True, multiplying=False)
            add_last(PAIRS * CHUNKS - 1, 1)
            combine(PAIRS * CHUNKS - 1, 1)
            low_x2t(PAIRS * CHUNKS - 1)

        @block.tensor
        def _(pe):
            def layer0(m, t):
                if t == TENSOR_TILES[0] and not is_zero(m):
                    pe.wait_ge(x1_stored, m)
                parts = PK if t < QT - 1 else QT_LAST
                if t in SPLIT_TILES:
                    i = SPLIT_TILES.index(t)
                    pe.wait_ge(products_lo_ready, len(SPLIT_TILES) * m + i + 1)
                    passes = ((w0_hi[0:parts, i, :], products_hi[0:parts, i, :]),
                              (w0_lo[0:parts, i, :], products_hi[0:parts, i, :]),
                              (w0_hi[0:parts, i, :], products_lo[0:parts, i, :]))
                else:
                    wait_product(pe, m, t)
                    passes = ((w0_sb[0:parts, t, :], products[0:parts, t, :]),)
                for step, (w, x) in enumerate(passes):
                    mm = nc.tensor.matmul(quad_ps[:, :], w, x, start=(t == TENSOR_TILES[0] and step == 0),
                                          stop=(t == TENSOR_TILES[-1] and step == len(passes) - 1))
                mm.then_inc(products_used, 1)

            def wait_for_xrow(m):
                pe.wait_ge(xrow_loaded, 16 * (m + 1))
                if not is_zero(m):
                    pe.wait_ge(xt_ready, PAIRS * m)

            def transposes(m):
                for i in range(BLKS):
                    mm = nc.tensor.transpose(xt_ps[:, FIELDS * i:FIELDS * (i + 1)],
                                             xrow[:, 128 * i:128 * (i + 1)], ident[0:FIELDS, 0:FIELDS])
                mm.then_inc(transposed, 1)

            def wait_left(q, s, g):
                if s == 0:
                    pe.wait_ge(vector_added, FIELDS * q + fields_of(g)[-1] + 1)
                else:
                    pe.wait_ge(staged_ready, GROUPS * q + g + 1)

            def layer1(q, pair, s, g):
                cols = slice(128 * (2 * pair + s), 128 * (2 * pair + s + 1))
                if g == 0 and s == 0:
                    pe.wait_ge(x1_lo_ready, q + 1)
                if g >= RING:
                    wait_left(q, s, g - RING)
                elif not is_zero(q):
                    wait_left(q - 1, s, GROUPS - RING + g)
                fields = slice(fields_of(g)[0], fields_of(g)[-1] + 1)
                bank = a_ps[s][g % RING][:, 0:H * len(fields_of(g))]
                for step, (x, w) in enumerate(((x1_hi, w1_hi), (x1_hi, w1_lo), (x1_lo, w1_hi))):
                    mm = nc.tensor.matmul(bank, x[:, cols], w[:, fields, :].rearrange("p j h -> p (j h)"),
                                          start=(step == 0), stop=(step == 2))
                mm.then_inc(filled[s], 1)

            def g_block(q, pair, s):
                if s == 0:
                    pe.wait_ge(diag_lo_ready, q + 1)
                    pe.wait_ge(x2t_lo_ready, q + 1)
                if not (is_zero(q) and s == 0):
                    pe.wait_ge(g_stored, 2 * q + s)
                for step, (w, x) in enumerate(((x2t_hi, diag_hi), (x2t_lo, diag_hi), (x2t_hi, diag_lo))):
                    mm = nc.tensor.matmul(g_ps[:, 0:(FIELDS + 1) * BLK_B], w[:, s, :],
                                          x[:, 2 * pair + s, :, :].rearrange("p b j -> p (b j)"),
                                          start=(step == 0), stop=(step == 2))
                mm.then_inc(g_ready, 1)

            def layer2(part):
                c0, c1 = PARTS[part]
                base = 0 if c0 < HALF_CHUNKS else HB
                pe.wait_ge(g_stored, BLKS * c1)
                if part == 0:
                    pe.wait_ge(late_loaded, 16 * (3 + HALF_CHUNKS))
                else:
                    pe.wait_ge(z3_stored, part)
                for j in range(FIELDS):
                    mm = nc.tensor.matmul(z3_ps[:, c0 * CB:c1 * CB], w2_sb[:, j, :],
                                          g_sb[:, j, c0 * CB - base:c1 * CB - base],
                                          start=(j == 0), stop=(j == FIELDS - 1))
                mm.then_inc(z3_ready, 1)

            def body(n, first=False, last=False, then=None):
                for pair in range(PAIRS):
                    q = PAIRS * n + pair
                    if pair == 1 and then is not None:
                        then()
                    for g in range(GROUPS):
                        layer1(q, pair, 0, g)
                        if not last and pair == 1 and g == TRANSPOSE_AT:
                            wait_for_xrow(n + 1)
                        layer1(q, pair, 1, g)
                        if not last and g in L0_PRODUCT_AT[pair]:
                            layer0(n + 1, L0_PRODUCT_AT[pair][g])
                        if not last and pair == 1 and g == TRANSPOSE_AT:
                            transposes(n + 1)
                        if g in G_AT and not (first and pair == 0):
                            g_block(q - 1, 1 - pair, G_AT[g])

            pe.wait_ge(w0_ready, 1)
            for t in TENSOR_TILES:
                layer0(0, t)
            pe.wait_ge(small_loaded, 64)
            wait_for_xrow(0)
            transposes(0)
            pe.wait_ge(w1_lo_ready, 3)
            body(0, first=True)
            with pe.Fori(1, HALF_CHUNKS) as n:
                body(n)
            body(HALF_CHUNKS, then=lambda: layer2(0))
            with pe.Fori(HALF_CHUNKS + 1, CHUNKS - 1) as n:
                body(n)
            body(CHUNKS - 1, last=True, then=lambda: layer2(1))
            banks = [quad_ps, xt_ps, a_ps[0][0], a_ps[0][1]]
            last_q = PAIRS * CHUNKS - 1
            pe.wait_ge(mlp_loaded, 16 * 4)
            pe.wait_ge(z1_summed, CHUNKS)
            wait_left(last_q, 0, GROUPS - 1)

            def mlp1(mt, rows):
                cols = slice(128 * mt, 128 * (mt + 1))
                return nc.tensor.matmul(banks[mt][:, :], wt1_sb[:, rows, cols], z[:, rows, :],
                                        start=False, stop=(rows == 2))

            for mt in range(N1 // 128):
                nc.tensor.matmul(banks[mt][:, :], wt1c_sb[:, 128 * mt:128 * (mt + 1)], ctx_sb[:, :],
                                 start=True, stop=False)
                mlp1(mt, 0)
            for s in range(2):
                g_block(last_q, 1, s)
            layer2(2)
            pe.wait_ge(g_stored, BLKS * CHUNKS)
            for mt in range(N1 // 128):
                mlp1(mt, 1)
            pe.wait_ge(z3_stored, 3)
            for mt in range(N1 // 128):
                mlp1(mt, 2).then_inc(mlp_ready, 1)
            for mt in range(N2 // 128):
                for kt in range(N1 // 128):
                    if mt == 0:
                        pe.wait_ge(mlp_stored, kt + 1)
                    mm = nc.tensor.matmul(a_ps[1][mt][:, :], wt2_sb[:, kt, 128 * mt:128 * (mt + 1)], h1[:, kt, :],
                                          start=(kt == 0), stop=(kt == N1 // 128 - 1))
                mm.then_inc(mlp_ready, 1)
            for kt in range(N2 // 128):
                pe.wait_ge(mlp_stored, N1 // 128 + kt + 1)
                mm = nc.tensor.matmul(g_ps[0:1, :], wt3_sb[:, kt:kt + 1], h2[:, kt, :],
                                      start=(kt == 0), stop=(kt == N2 // 128 - 1))
            mm.then_inc(mlp_ready, 1)

        @block.scalar
        def _(act):
            def store_x1(m):
                if not is_zero(m):
                    act.wait_ge(x1_lo_ready, PAIRS * m)
                    act.wait_ge(z1_summed, m)
                act.wait_ge(products_used, QT * (m + 1))
                nc.scalar.activation(x1[:, :], quad_ps[:, :], ACT.Identity, bias=bias_sb[:, 0:1]
                                     ).then_inc(x1_stored, 1)

            def high_x1(n, pair):
                q = PAIRS * n + pair
                cols = slice(PW * pair, PW * (pair + 1))
                act.wait_ge(x1_stored, n + 1)
                if not (isinstance(n, int) and n == 0):
                    act.wait_ge(filled[1], GROUPS * (q - 1))
                nc.scalar.copy(x1_hi[:, cols], x1[:, cols]).then_inc(x1_hi_ready, 1)

            def store_xt(n, pair):
                q = PAIRS * n + pair
                blks = slice(2 * pair, 2 * pair + 2)
                act.wait_ge(transposed, n + 1)
                if not (isinstance(n, int) and n == 0):
                    act.wait_ge(vector_added, FIELDS * (q - 1))
                    act.wait_ge(diag_copied[pair], 16 * BLK_B * n)
                nc.scalar.copy(xt[:, blks, :], xt_ps[:, 2 * pair * FIELDS:2 * (pair + 1) * FIELDS]
                               .rearrange("p (i j) -> p i j", j=FIELDS)).then_inc(xt_ready, 1)

            def high_product(m, t):
                wait_product(act, m, t)
                nc.scalar.copy(products_hi[:, SPLIT_TILES.index(t), :], products[0:PK, t, :]
                               ).then_inc(products_hi_ready, 1)

            def high_diag(n, pair):
                q = PAIRS * n + pair
                blks = slice(2 * pair, 2 * pair + 2)
                act.wait_ge(diag_copied[pair], 16 * BLK_B * (n + 1))
                if not (isinstance(q, int) and q < 2):
                    act.wait_ge(g_ready, 2 * (q - 1))
                nc.scalar.copy(diag_hi[:, blks, :, :], diag[:, blks, :, :]).then_inc(diag_hi_ready, 1)

            def stage(q, pair, g):
                act.wait_ge(filled[1], GROUPS * q + g + 1)
                if g == 0:
                    act.wait_ge(xt_ready, q + 1)
                    target = sums[:, pair, :, :]
                    if not (isinstance(q, int) and q < 2):
                        act.wait_ge(folded, q - 1)
                elif g == GROUPS - 1:
                    target = staged_last
                    if not is_zero(q):
                        act.wait_ge(last_added, q)
                else:
                    target = staged[:, (g - 1) % STAGES, :, :]
                    if g > STAGES:
                        act.wait_ge(pool_added, ADDS * q + g - STAGES)
                    elif not is_zero(q):
                        act.wait_ge(pool_added, ADDS * q + g - STAGES)
                for j in fields_of(g):
                    last = nc.scalar.activation(target[:, j % GF, :], a_ps[1][g % RING][:, H * (j % GF):H * (j % GF + 1)],
                                                ACT.Copy, scale=xt[:, 2 * pair + 1, j:j + 1])
                last.then_inc(staged_ready, 1)

            def high_x2t(q):
                act.wait_ge(x2t_ready, q + 1)
                if not is_zero(q):
                    act.wait_ge(g_ready, 2 * q)
                nc.scalar.copy(x2t_hi[:, :, :], x2t[:, :, :]).then_inc(x2t_hi_ready, 1)

            def store_g(n, pair, s, half):
                q = PAIRS * n + pair
                col = n * CB + (2 * pair + s) * BLK_B
                act.wait_ge(g_ready, 2 * q + s + 1)
                g = g_ps[:, 0:(FIELDS + 1) * BLK_B].rearrange("p (b j) -> p j b", b=BLK_B)
                nc.scalar.copy(g_sb[:, :, bass.ds(col - half * HB, BLK_B)], g[:, 0:FIELDS, :])
                nc.scalar.copy(z[:, 1, bass.ds(col, BLK_B)], g[:, FIELDS, :]).then_inc(g_stored, 1)

            def store_z3(part):
                cols = slice(PARTS[part][0] * CB, PARTS[part][1] * CB)
                act.wait_ge(z3_ready, part + 1)
                nc.scalar.activation(z[:, 2, cols], z3_ps[:, cols], ACT.Identity, bias=bias2d[:, :]
                                     ).then_inc(z3_stored, 1)

            def body(n, half, first=False, last=False, half_before=None, part=None):
                for pair in range(PAIRS):
                    q = PAIRS * n + pair
                    for g in range(GROUPS):
                        stage(q, pair, g)
                        if not last and pair == 0 and g in L0_HIGH_AT:
                            high_product(n + 1, L0_HIGH_AT[g])
                        if g == COMBINE_AT + 2 and not (first and pair == 0):
                            high_x2t(q - 1)
                        if pair == 0:
                            if g == 0:
                                high_x1(n, 1)
                            if g == 2:
                                store_xt(n, 1)
                            if g in (7, 9) and not first:
                                store_g(n - 1, 1, g == 9, half if half_before is None else half_before)
                        else:
                            if g == 0 and part is not None:
                                store_z3(part)
                            if g in (7, 9):
                                store_g(n, 0, g == 9, half)
                            if g == 5 and not last:
                                store_x1(n + 1)
                            if g == 6 and not last:
                                high_x1(n + 1, 0)
                            if g == 8 and not last:
                                store_xt(n + 1, 0)
                        if g == 4:
                            high_diag(n, pair)

            act.wait_ge(w0_folded, 1)
            for i, t in enumerate(SPLIT_TILES):
                last = nc.scalar.copy(w0_hi[:, i, :], w0_sb[:, t, :])
            last.then_inc(w0_hi_ready, 1)
            act.wait_ge(small_loaded, 64)
            act.wait_ge(diag_zeroed, 1)
            for i in range(BLKS):
                last = nc.scalar.copy(diag[:, i, :, FIELDS], mask[:, :])
            last.then_inc(diag_set, 1)
            act.wait_ge(w1_loaded, 16)
            for part in range(3):
                j0, j1 = FIELDS * part // 3, FIELDS * (part + 1) // 3
                nc.scalar.copy(w1_hi[:, j0:j1, :], w1_sb[:, j0:j1, :]).then_inc(w1_hi_ready, 1)
            for t in SPLIT_TILES:
                high_product(0, t)
            act.wait_ge(bias_ready, 1)
            store_x1(0)
            high_x1(0, 0)
            store_xt(0, 0)
            act.wait_ge(w1_lo_ready, 3)
            body(0, 0, first=True)
            with act.Fori(1, HALF_CHUNKS) as n:
                body(n, 0)
            body(HALF_CHUNKS, 1, half_before=0, part=0)
            with act.Fori(HALF_CHUNKS + 1, CHUNKS - 1) as n:
                body(n, 1)
            body(CHUNKS - 1, 1, last=True, part=1)
            high_x2t(PAIRS * CHUNKS - 1)
            for s in range(2):
                store_g(CHUNKS - 1, 1, s, 1)
            store_z3(2)
            banks = [quad_ps, xt_ps, a_ps[0][0], a_ps[0][1]]
            for mt in range(N1 // 128):
                act.wait_ge(mlp_ready, mt + 1)
                nc.scalar.activation(h1[:, mt, :], banks[mt][:, :], ACT.Relu, bias=bt1_sb[:, mt:mt + 1]
                                     ).then_inc(mlp_stored, 1)
            for mt in range(N2 // 128):
                act.wait_ge(mlp_ready, N1 // 128 + mt + 1)
                nc.scalar.activation(h2[:, mt, :], a_ps[1][mt][:, :], ACT.Relu, bias=bt2_sb[:, mt:mt + 1]
                                     ).then_inc(mlp_stored, 1)
            act.wait_ge(mlp_ready, N1 // 128 + N2 // 128 + 1)
            nc.scalar.copy(y_sb[:, :], g_ps[0:1, :]).then_inc(mlp_stored, 1)


def kernel(**inputs):
    import concourse.bacc as bacc
    from concourse.bass_utils import run_bass_kernel_spmd

    a = {k: np.asarray(v) for k, v in inputs.items()}
    ids = np.zeros((GATHERS * FPG, B), np.int32)
    ids[:FIELDS] = a["ids"].T
    ids = ids.reshape(GATHERS, FPG, CHUNKS, CB).transpose(1, 3, 2, 0).reshape(128, CHUNKS, GATHERS)
    first = np.zeros(GATHERS * FPG, np.int32)
    first[:FIELDS] = np.concatenate([[0], np.cumsum(VOCABS)[:-1]])
    bases = np.repeat(first.reshape(GATHERS, FPG).T, CB, axis=0)
    tables = np.concatenate([a[f"tbl_{f}"] for f in range(FIELDS)], axis=0)
    w0 = a["L0_rec_W0"].reshape(H, FIELDS, FIELDS)
    j = np.arange(FIELDS)[None, :, None]
    s = np.arange(SPT)[:, None, None] + SPT * np.arange(QT)[None, None, :]
    k = (j + s) % FIELDS
    j = np.broadcast_to(j, k.shape)
    w0a = w0[:, j, k].transpose(1, 2, 3, 0).reshape(PK, QT, H)
    w0b = w0[:, k, j].transpose(1, 2, 3, 0).reshape(PK, QT, H).copy()
    w0b[:FIELDS, 0] = 0
    by_j = lambda w: w.reshape(H, FIELDS, H).transpose(2, 1, 0)
    mask = (np.arange(128)[:, None] // D == np.arange(BLK_B)[None, :]).astype(np.float32)
    arrays = {
        "ids": ids, "bases": bases, "tables": tables, "w0a": w0a, "w0b": w0b,
        "w1": by_j(a["L0_rec_W1"]), "w2": by_j(a["L0_rec_W2"]),
        "biases": np.stack([a[f"L0_rec_b{i}"] for i in range(3)], axis=1),
        "b1_row": a["L0_rec_b1"][None, :],
        "ctx_in": a["dense_ctx"].T,
        "wt1": a["W_top1"][:3 * 128].reshape(3, 128, N1).transpose(1, 0, 2), "wt1c": a["W_top1"][3 * 128:],
        "bt1": a["b_top1"].reshape(N1 // 128, 128).T,
        "wt2": a["W_top2"].reshape(N1 // 128, 128, N2).transpose(1, 0, 2),
        "bt2": a["b_top2"].reshape(N2 // 128, 128).T, "wt3": a["W_top3"].reshape(N2 // 128, 128).T,
        "ident_in": np.eye(128, dtype=np.float32), "mask_in": mask,
    }
    arrays = {f"{k}_dram": np.ascontiguousarray(v) for k, v in arrays.items()}
    nc = bacc.Bacc("TRN2", target_bir_lowering=False, num_devices=1)
    aps = {n.removesuffix("_dram"): nc.dram_tensor(n, v.shape, mybir.dt.from_np(v.dtype), kind="ExternalInput").ap()
           for n, v in arrays.items()}
    aps["x_rows"] = nc.dram_tensor("x_rows", (X_ROWS, COLS), F32, kind="Internal").ap()
    aps["out"] = nc.dram_tensor("out_dram", (1, B), F32, kind="ExternalOutput").ap()
    build(nc, **aps)
    r = run_bass_kernel_spmd(nc, [arrays], core_ids=[0])
    return r.results[0]["out_dram"].reshape(B, 1)
```
